# Optimizing a Trainium2 kernel written in Bass

```python
import numpy as np
import jax
import jax.numpy as jnp

def _softmax(x, axis=-1):
    return jax.nn.softmax(x, axis=axis)

def _gelu(x):
    return jax.nn.gelu(x, approximate=True)

def _silu(x):
    return jax.nn.silu(x)

def _sigmoid(x):
    return jax.nn.sigmoid(x)

def _layernorm(x, axis=-1, eps=1e-05):
    m = jnp.mean(x, axis=axis, keepdims=True)
    v = jnp.var(x, axis=axis, keepdims=True)
    return (x - m) / jnp.sqrt(v + eps)

def _scatter_add(tgt, idx, src, axis=0):
    return tgt.at[idx].add(src)

def _segment_sum(src, seg, n):
    return jax.ops.segment_sum(src, seg, n)
kernel_name = 'mk_adj_resnorm_d2_adj_r2_fd3bb1'

def setup_inputs(seed: int=0):
    np.random.seed(seed)
    _w = jnp.asarray

    def _rec_inputs():
        import jax
        import jax.numpy as jnp
        _gk = jax.random.key(seed)
        x = -9.806e-05 + 1 * jax.random.normal(jax.random.fold_in(_gk, 1), (4096, 64), jnp.float32)
        _a = jax.random.bernoulli(jax.random.fold_in(_gk, 2), 0.000976562, (4096, 4096))
        adj = _a.astype(jnp.int32)
        return (x, adj)
    x, adj = _rec_inputs()

    def _L0_gnn_setup():
        import jax, jax.numpy as jnp
        import numpy as np
        N = 4096
        D = 64
        NEG_INF = -9000000000000000.0
        LEAKY_SLOPE = 0.01
        key = jax.random.key(seed)
        k1, k2, k3 = jax.random.split(key, 3)
        h = jax.random.normal(k1, (N, D), dtype=jnp.float32)
        adj = jax.random.randint(k2, (N, N), 0, 2, dtype=jnp.int32)
        bound = float(np.sqrt(6.0 / (2 * D + 1)))
        a = jax.random.uniform(k3, (2 * D, 1), dtype=jnp.float32, minval=-bound, maxval=bound)
        return {'h': h, 'adj': adj, 'a': a}
    _L0_gnn_all = _L0_gnn_setup()
    _L0_gnn_in = {k: v for k, v in _L0_gnn_all.items() if k in ('a',)}
    del _L0_gnn_all

    def _L1_gnn_setup():
        import jax, jax.numpy as jnp
        import numpy as np
        N = 6144
        IN_C = 64
        OUT_C = 64
        NEG_INF = -1000000000.0
        key = jax.random.key(seed)
        k1, k2, k3, k4 = jax.random.split(key, 4)
        x = jax.random.normal(k1, (N, IN_C), dtype=jnp.float32)
        edge_index = jax.random.randint(k2, (N, N), 0, 2, dtype=jnp.int32)
        weight_w = jax.random.normal(k3, (IN_C, OUT_C), dtype=jnp.float32) * (1.0 / np.sqrt(IN_C))
        weight_a = jax.random.normal(k4, (2 * OUT_C, 1), dtype=jnp.float32) * (1.0 / np.sqrt(OUT_C))
        bias = jnp.zeros((OUT_C,), dtype=jnp.float32)
        return {'x': x, 'edge_index': edge_index, 'weight_w': weight_w, 'weight_a': weight_a, 'bias': bias}
    _L1_gnn_all = _L1_gnn_setup()
    _L1_gnn_in = {k: v for k, v in _L1_gnn_all.items() if k in ('weight_w', 'weight_a', 'bias')}
    del _L1_gnn_all
    return {'x': x, 'adj': adj, 'L0_gnn_a': _L0_gnn_in['a'], 'L1_gnn_weight_w': _L1_gnn_in['weight_w'], 'L1_gnn_weight_a': _L1_gnn_in['weight_a'], 'L1_gnn_bias': _L1_gnn_in['bias']}

def reference(x, adj, L0_gnn_a, L1_gnn_weight_w, L1_gnn_weight_a, L1_gnn_bias):
    import jax
    import jax.numpy as jnp

    def _L0_gnn_ref(h, adj, a):
        import jax, jax.numpy as jnp
        import numpy as np
        N = 4096
        D = 64
        NEG_INF = -9000000000000000.0
        LEAKY_SLOPE = 0.01
        a1 = a[:D, 0]
        a2 = a[D:, 0]
        src = h @ a1
        dst = h @ a2
        e = src[:, None] + dst[None, :]
        e = jnp.where(e > 0, e, LEAKY_SLOPE * e)
        e = jnp.where(adj > 0, e, NEG_INF)
        attention = jax.nn.softmax(e, axis=1)
        h_prime = attention @ h
        return h_prime

    def _L1_gnn_ref(x, edge_index, weight_w, weight_a, bias):
        import jax, jax.numpy as jnp
        import numpy as np
        N = 6144
        IN_C = 64
        OUT_C = 64
        NEG_INF = -1000000000.0
        wh = x @ weight_w
        a_src = weight_a[:OUT_C, 0]
        a_dst = weight_a[OUT_C:, 0]
        e = (wh @ a_src)[:, None] + (wh @ a_dst)[None, :]
        e = jax.nn.leaky_relu(e, negative_slope=0.01)
        scores = jnp.where(edge_index > 0, e, NEG_INF)
        attention = jax.nn.softmax(scores, axis=1)
        out = attention @ wh
        return out + bias
    x = _layernorm(x + _L0_gnn_ref(x, adj, L0_gnn_a), axis=-1)
    x = _layernorm(x + _L1_gnn_ref(x, adj, L1_gnn_weight_w, L1_gnn_weight_a, L1_gnn_bias), axis=-1)
    return x

_drawn_inputs = setup_inputs


def setup_inputs(seed=0):
    import zlib

    import numpy as np

    out = dict(_drawn_inputs(seed))
    spreads = {'L1_gnn_bias': (0.0, 0.1)}
    factors = {}
    for name, (base, spread) in spreads.items():
        noise = np.random.default_rng([zlib.crc32(name.encode()), seed]).standard_normal(out[name].shape)
        drawn = base * np.exp(spread * noise) if base else spread * noise
        out[name] = jnp.asarray(drawn.astype(out[name].dtype))
    for name, factor in factors.items():
        out[name] = (out[name] * factor).astype(out[name].dtype)
    return out
```

```python
from contextlib import ExitStack

import numpy as np

import concourse.bass as bass
from concourse import mybir

ALU = mybir.AluOpType
ACT = mybir.ActivationFunctionType
AX = mybir.AxisListType.X
F32 = mybir.dt.float32
BF16 = mybir.dt.bfloat16
FP8 = mybir.dt.float8e4
I8 = mybir.dt.int8
U8 = mybir.dt.uint8
I32 = mybir.dt.int32
U32 = mybir.dt.uint32

P = 128
Q = 32
BYTES = 4
SLOPE = 0.01
EPS = 1e-5


def gat_kernel(nc, x, adj, a0, w1, a1, bias1, ident, out):
    N, D = x.shape
    IB = N // P
    SUP = 512
    NS = N // SUP
    RB = SUP // P
    GR = SUP // Q
    NA = P // Q
    NB = N // NA // P
    TILES = NB * BYTES
    GB = 2
    NG = NB // GB
    GT = GB * BYTES
    GW = GB * GR * Q
    GN = GW * BYTES
    JC = GB * P
    E = D + 1
    PARTS = 3
    XW = PARTS * E
    KEEP = NG // 2
    RING = 2
    CODE = [0x20, 0x40]
    BIT = [0x20202020, 0x40404040]
    RESCALE = 2.0 ** -4
    FREE_AT_FIRST = RING * RB
    WH_BANK = 7

    ctx = ExitStack()
    with ctx:
        def sb(name, shape, dt):
            return ctx.enter_context(nc.sbuf_tensor(name, shape, dt))

        def sem(name):
            return ctx.enter_context(nc.semaphore(name))

        kept = sb("kept", [P, NS * KEEP * GN], U8)
        stage = sb("stage", [P, NG, GR * JC], I32)
        narrow = sb("narrow", [P, GN], U8)
        neg = sb("neg", [P, RING, GN], U8)
        pos = sb("pos", [P, RING, GN], U8)
        xT = sb("xT", [D, N], F32)
        xn = sb("xn", [P, IB, D], F32)
        xy0 = sb("xy0", [P, TILES, 2, PARTS, E], BF16)
        red = sb("red", [P, RB, 2, E], F32)
        num = sb("num", [P, RB, E], F32)
        y = num[:, :, 0:D]
        ysq = red[:, :, 0, 0:D]
        x1s = sb("x1s", [P, RB, D], F32)
        small = sb("small", [P, 8, RB], F32)
        idf = sb("idf", [P, P], F32)
        onesN = sb("onesN", [P, P], F32)
        one_row = sb("one_row", [1, P], F32)
        minus_half = sb("minus_half", [P, RB], F32)
        acol = sb("acol", [D, 4], F32)
        wext0 = sb("wext0", [D, E], F32)
        wext1 = sb("wext1", [D, E], F32)
        wT = sb("wT", [D, D], F32)
        arep = sb("arep", [D, 2, P], F32)
        dcol = sb("dcol", [P, 2, TILES], F32)
        scol = sb("scol", [P, 2, IB], F32)
        mcol = sb("mcol", [P, 8], F32)
        ab = sb("ab", [P, 2, 2, IB], F32)
        wts = sb("wts", [P, 2, 2, TILES], F32)
        meanv = sb("meanv", [P, 2, D], F32)
        hsum = sb("hsum", [P, D], F32)
        biasr = sb("biasr", [P, D], F32)

        stage_f = stage[:, :, :].rearrange("p s n -> p (s n)").bitcast(F32)
        TAB = TILES * E
        kept_f = kept[:, :].bitcast(F32)
        tail = NS * KEEP * GN // 4
        wh = [kept_f[:, tail - TAB:tail].rearrange("p (t f) -> p t f", f=E),
              stage_f[:, 0:TAB].rearrange("p (t f) -> p t f", f=E)]
        prod = [kept_f[:, tail - 3 * TAB:tail - TAB].rearrange("p (c t f) -> p c t f", c=2, f=E),
                stage_f[:, TAB:3 * TAB].rearrange("p (c t f) -> p c t f", c=2, f=E)]
        XYW = TILES * 2 * XW // 2
        xy1 = stage_f[:, 3 * TAB:3 * TAB + XYW].bitcast(BF16).rearrange("p (t c k f) -> p t c k f", c=2, k=PARTS, f=E)
        xy = [xy0[:, :, :, :, :], xy1]

        acc = ctx.enter_context(nc.psum_tensor("acc", [P, RB, 512], F32))
        srow = ctx.enter_context(nc.psum_tensor("srow", [P, 2 * 512], F32))
        flip = ctx.enter_context(nc.psum_tensor("flip", [P, 512], F32))
        misc = ctx.enter_context(nc.psum_tensor("misc", [P, 512], F32))

        loaded = [sem(f"loaded{g}") for g in range(NG)]
        s_x = sem("s_x")
        s_w = sem("s_w")
        s_bias = sem("s_bias")
        const_ready = sem("const_ready")
        w_ready = sem("w_ready")
        xT_psum = sem("xT_psum")
        xT_ready = sem("xT_ready")
        tab_psum = sem("tab_psum")
        tab_ready = sem("tab_ready")
        max_step = sem("max_step")
        max_psum = sem("max_psum")
        shift_ready = sem("shift_ready")
        exp_ready = sem("exp_ready")
        dve_pre = sem("dve_pre")
        pool_pre = sem("pool_pre")
        weights_ready = sem("weights_ready")
        x_parts = sem("x_parts")
        y_parts = sem("y_parts")
        srow_ready = sem("srow_ready")
        narrowed = sem("narrowed")
        turned_ready = sem("turned_ready")
        turned_kept = sem("turned_kept")
        signs_ready = sem("signs_ready")
        neg_ready = sem("neg_ready")
        pos_ready = sem("pos_ready")
        pe_turn = sem("pe_turn")
        act_turn = sem("act_turn")
        pool_turn = sem("pool_turn")
        products = sem("products")
        acc_read = sem("acc_read")
        epi = sem("epi")
        var_ready = sem("var_ready")
        std_ready = sem("std_ready")
        x1_ready = sem("x1_ready")
        x1_turned = sem("x1_turned")
        x1_kept = sem("x1_kept")
        out_ready = sem("out_ready")
        stored = sem("stored")

        block = ctx.enter_context(nc.Block())

        xT_blocks = xT[:, :].rearrange("d (h r a i) -> d h r a i", h=2, r=RB, a=NA)

        def xT_at(s):
            if isinstance(s, int):
                return xT_blocks[:, s % 2, :, s // 2, :]
            return xT_blocks[:, bass.ds(s % 2, 1), :, bass.ds(s // 2, 1), :].rearrange("d h r a i -> d (h r a) i")

        def kept_at(s, g):
            return kept[:, bass.ds(s * (KEEP * GN) + (g % KEEP) * GN, GN)]

        @block.sync
        def _(sp):
            sp.sem_inc(stored, 16)
            sp.dma_start(idf[:, :], ident).then_inc(s_x, 16)
            sp.dma_start(xn[:, :, :], x.rearrange("(b p) d -> p b d", p=P)).then_inc(s_x, 16)
            sp.dma_start(acol[:, 0:1], a0[0:D, :]).then_inc(s_w, 16)
            sp.dma_start(acol[:, 1:2], a0[D:2 * D, :]).then_inc(s_w, 16)
            sp.dma_start(acol[:, 2:3], a1[0:D, :]).then_inc(s_w, 16)
            sp.dma_start(acol[:, 3:4], a1[D:2 * D, :]).then_inc(s_w, 16)
            sp.dma_start(wext1[:, 0:D], w1).then_inc(s_w, 16)
            sp.dma_start(biasr[:, :], bias1.rearrange("(o d) -> o d", o=1).broadcast_to((P, D))).then_inc(s_bias, 16)

            def load(s, g):
                rows = adj[bass.ds(s * SUP, SUP), :].rearrange("(g p) j -> p g j", p=Q)
                for a in range(NA):
                    c = a * (N // NA) + g * JC
                    sp.dma_start(stage[Q * a:Q * a + Q, g, :].rearrange("p (g j) -> p g j", j=JC),
                                 rows[:, :, c:c + JC]).then_inc(loaded[g], 16)

            for g in range(NG):
                load(0, g)
            with sp.Fori(1, NS) as s:
                for g in range(NG):
                    sp.wait_ge(narrowed, (s - 1) * NG + g + 1)
                    load(s, g)

            with sp.Fori(0, NS) as s:
                sp.wait_ge(out_ready, s + 1)
                sp.dma_start(out[bass.ds(s * SUP, SUP), :].rearrange("(b p) d -> p b d", p=P),
                             x1s[:, :, :]).then_inc(stored, 16)
            sp.wait_ge(stored, 16 * (NS + 1))

        @block.tensor
        def _(pe):
            pe.sem_inc(x1_turned, 1)
            pe.sem_inc(products, FREE_AT_FIRST)
            pe.wait_ge(s_x, 32)
            pe.wait_ge(s_w, 80)
            nc.tensor.transpose(misc[0:D, 0:D], wext1[:, 0:D], idf[0:D, 0:D]).then_inc(max_psum, 1)
            pe.wait_ge(w_ready, 1)
            nc.tensor.matmul(misc[0:D, 64:66], wT[:, :], acol[:, 2:4], start=True, stop=True).then_inc(max_psum, 1)
            for t in range(NS):
                if t >= RB:
                    pe.wait_ge(xT_ready, t - RB + 1)
                for b in range(RB):
                    last = nc.tensor.transpose(acc[0:D, t % RB, b * P:(b + 1) * P], xn[:, t * RB + b, :], idf[:, :])
                last.then_inc(xT_psum, 1)

            def score_row(layer, s):
                nc.tensor.matmul(srow[:, bass.ds((s % 2) * 512, 512)], arep[:, layer, :], xT_at(s),
                                 start=True, stop=True).then_inc(srow_ready, 1)

            def tables(layer):
                pe.wait_ge(w_ready, 3)
                pe.wait_ge(xT_ready, NS * (layer + 1))
                score_row(layer, 0)
                wx = [wext0, wext1][layer]
                av = [acol[:, 0:1], arep[:, 1, 0:1]][layer]
                if layer:
                    pe.wait_ge(acc_read, NS * RB + RB)
                xcols = xT[:, :].rearrange("d (b c e) -> d b e c", b=NB, e=BYTES)
                for t in range(TILES):
                    b = t // WH_BANK
                    dst = acc[:, b, :] if b < RB else misc[:, :]
                    c = (t % WH_BANK) * E
                    last = nc.tensor.matmul(dst[:, c:c + E], xcols[:, t // BYTES, t % BYTES], wx[:, :],
                                            start=True, stop=True)
                    if t % WH_BANK == WH_BANK - 1 or t == TILES - 1:
                        last.then_inc(tab_psum, 1)
                for b in range(IB):
                    last = nc.tensor.matmul(flip[:, b:b + 1], xT_at(b // RB)[:, b % RB, :], av, start=True, stop=True)
                last.then_inc(tab_psum, 1)
                pe.wait_ge(max_step, 3 * layer + 1)
                nc.tensor.transpose(flip[0:1, 128:256], mcol[:, 0:1], idf[:, :]).then_inc(max_psum, 1)
                pe.wait_ge(max_step, 3 * layer + 2)
                nc.tensor.matmul(srow[:, 512:512 + D], onesN[:, :], hsum[:, :], start=True, stop=True).then_inc(max_psum, 1)
                pe.wait_ge(max_step, 3 * layer + 3)
                nc.tensor.matmul(flip[:, 256:257], one_row[:, :], mcol[0:1, 1:2], start=True, stop=True).then_inc(max_psum, 1)

            def granule(layer, s, g):
                k = (layer * NS + s) * NG + g
                pe.wait_ge(neg_ready, k + 1)
                pe.wait_ge(pos_ready, k + 1)
                pe.sem_inc(pe_turn, 1)
                pe.wait_ge(x_parts, layer * NG + g + 1)
                pe.wait_ge(y_parts, layer * NG + g + 1)
                masks = [m[:, g % RING, :].bitcast(FP8).rearrange("p (b i e) -> p b e i", b=GB, e=BYTES) for m in (pos, neg)]
                for r in range(RB):
                    if g == 0:
                        pe.wait_ge(acc_read, (layer * NS + s) * RB + r + 1)
                    if g == 0:
                        pe.sem_inc(pe_turn, 1)
                    for t in range(GT):
                        for c in range(2):
                            last = nc.tensor.matmul(
                                acc[:, r, c * XW:(c + 1) * XW], masks[c][:, t // BYTES, t % BYTES, r * P:(r + 1) * P],
                                xy[layer][:, g * GT + t, c].rearrange("p k f -> p (k f)"),
                                start=(g == 0 and t == 0 and c == 0), stop=(g == NG - 1 and t == GT - 1),
                                skip_group_check=True)
                    last.then_inc(products, 1)

            def turn_x1(s):
                pe.wait_ge(x1_ready, s + 1)
                pe.wait_ge(xT_ready, NS + s)
                pe.sem_inc(pe_turn, 1)
                for b in range(RB):
                    last = nc.tensor.transpose(flip[0:D, b * P:(b + 1) * P], x1s[:, b, :], idf[:, :])
                last.then_inc(x1_turned, 1)

            for layer in range(2):
                tables(layer)
                granule(layer, 0, 0)
                granule(layer, 0, 1)
                with pe.Fori(0, NS - 1) as s:
                    score_row(layer, s + 1)
                    granule(layer, s, 2)
                    granule(layer, s, 3)
                    granule(layer, s + 1, 0)
                    granule(layer, s + 1, 1)
                    if layer == 0:
                        turn_x1(s)
                granule(layer, NS - 1, 2)
                granule(layer, NS - 1, 3)
                if layer == 0:
                    turn_x1(NS - 1)

        @block.scalar
        def _(act):
            act.wait_ge(max_psum, 1)
            nc.scalar.copy(wT[:, :], misc[0:D, 0:D]).then_inc(w_ready, 1)
            for t in range(NS):
                act.wait_ge(xT_psum, t + 1)
                nc.scalar.copy(xT_at(t), acc[0:D, t % RB, :].rearrange("d (r i) -> d r i", r=RB)).then_inc(xT_ready, 1)

            def tables(layer):
                for b in range(RB + 1):
                    t0, t1 = b * WH_BANK, min((b + 1) * WH_BANK, TILES)
                    src = acc[:, b, 0:(t1 - t0) * E] if b < RB else misc[:, 0:(t1 - t0) * E]
                    act.wait_ge(tab_psum, (RB + 2) * layer + b + 1)
                    nc.scalar.copy(wh[layer][:, t0:t1, :].rearrange("p t f -> p (t f)"), src).then_inc(tab_ready, 1)
                act.wait_ge(tab_psum, (RB + 2) * (layer + 1))
                nc.scalar.copy(scol[:, layer, :], flip[:, 0:IB]).then_inc(tab_ready, 1)
                act.wait_ge(shift_ready, layer + 1)
                nc.scalar.activation(wts[:, layer, 0, :], dcol[:, layer, :], ACT.Exp, bias=mcol[:, 2:3]).then_inc(exp_ready, 1)
                nc.scalar.activation(wts[:, layer, 1, :], dcol[:, layer, :], ACT.Exp, bias=mcol[:, 3:4],
                                     scale=SLOPE).then_inc(exp_ready, 1)
                nc.scalar.activation(ab[:, layer, :, :], ab[:, layer, :, :], ACT.Exp).then_inc(exp_ready, 1)

            def signs(layer, s, g):
                k = (layer * NS + s) * NG + g
                if g == 0:
                    act.wait_ge(srow_ready, layer * NS + s + 1)
                act.wait_ge(products, (k + 1) * RB)
                act.sem_inc(act_turn, 1)
                o = neg[:, g % RING, :].bitcast(I8).rearrange("p (b i e) -> p b e i", b=GB, e=BYTES)
                for t in range(GT):
                    col = g * GT + t
                    last = nc.scalar.activation(o[:, t // BYTES, t % BYTES, :], srow[:, bass.ds((s % 2) * 512, 512)],
                                                ACT.Sign, bias=dcol[:, layer, col:col + 1])
                last.then_inc(signs_ready, 1)

            def copy_x1(s):
                act.wait_ge(x1_turned, s + 2)
                act.sem_inc(act_turn, 1)
                nc.scalar.copy(xT_at(s), flip[0:D, :].rearrange("d (r i) -> d r i", r=RB)).then_inc(xT_ready, 1)

            for layer in range(2):
                tables(layer)
                for g in range(3):
                    signs(layer, 0, g)
                with act.Fori(0, NS - 1) as s:
                    signs(layer, s, 3)
                    signs(layer, s + 1, 0)
                    signs(layer, s + 1, 1)
                    signs(layer, s + 1, 2)
                    if layer == 0:
                        copy_x1(s)
                signs(layer, NS - 1, 3)
                if layer == 0:
                    copy_x1(NS - 1)

        @block.vector
        def _(dve):
            dve.sem_inc(acc_read, RB)
            pre = [0]

            def step(ins):
                pre[0] += 1
                ins.then_inc(dve_pre, 1)
                dve.wait_ge(dve_pre, pre[0])

            nc.vector.memset(onesN[:, :], 1.0 / N).then_inc(const_ready, 1)
            nc.vector.memset(one_row[:, :], 1.0).then_inc(const_ready, 1)
            nc.vector.memset(minus_half[:, :], -0.5).then_inc(const_ready, 1)
            dve.wait_ge(s_x, 32)
            dve.wait_ge(s_w, 80)
            nc.vector.tensor_copy(wext0[:, 0:D], idf[0:D, 0:D])
            nc.vector.tensor_copy(wext0[:, D:E], acol[:, 1:2])
            nc.vector.tensor_copy(arep[:, 0, :], acol[:, 0:1].broadcast_to((D, P)))
            dve.wait_ge(max_psum, 2)
            nc.vector.tensor_copy(arep[:, 1, :], misc[0:D, 64:65].broadcast_to((D, P))).then_inc(w_ready, 1)
            nc.vector.tensor_copy(wext1[:, D:E], misc[0:D, 65:66]).then_inc(w_ready, 1)

            def tables(layer):
                w = wh[layer]
                dve.wait_ge(tab_ready, (RB + 2) * (layer + 1))
                step(nc.vector.tensor_copy(dcol[:, layer, :], w[:, :, D]))
                nc.vector.tensor_reduce(mcol[:, 0:1], dcol[:, layer, :], AX, ALU.max).then_inc(max_step, 1)
                nc.vector.tensor_reduce(hsum[:, :], w[:, :, 0:D].rearrange("p t f -> p f t"), AX, ALU.add).then_inc(max_step, 1)
                step(nc.vector.memset(w[:, :, D:E], 1.0))
                dve.wait_ge(max_psum, 3 + 3 * layer)
                nc.vector.tensor_reduce(mcol[0:1, 1:2], flip[0:1, 128:256], AX, ALU.max).then_inc(max_step, 1)
                dve.wait_ge(max_psum, 5 + 3 * layer)
                nc.vector.tensor_copy(meanv[:, layer, :], srow[:, 512:512 + D])
                step(nc.vector.tensor_scalar(mcol[:, 2:3], flip[:, 256:257], -1.0, None, ALU.mult))
                nc.vector.tensor_scalar(mcol[:, 3:4], mcol[:, 2:3], SLOPE, None, ALU.mult)
                step(nc.vector.tensor_scalar(scol[:, layer, :], scol[:, layer, :], mcol[:, 2:3], None, ALU.subtract))
                nc.vector.tensor_scalar(ab[:, layer, 0, :], scol[:, layer, :], 1 - SLOPE, 0.0, ALU.mult, ALU.min)
                nc.vector.tensor_scalar(ab[:, layer, 1, :], scol[:, layer, :], SLOPE - 1, 0.0, ALU.mult, ALU.min)\
                  .then_inc(shift_ready, 1)
                dve.wait_ge(exp_ready, 3 * (layer + 1))
                h = KEEP * GT
                nc.vector.tensor_scalar(wts[:, layer, :, h:TILES], wts[:, layer, :, h:TILES], RESCALE, None, ALU.mult)\
                  .then_inc(weights_ready, 1)
                dve.wait_ge(weights_ready, layer + 1)
                split_x(layer)

            def split_x(layer):
                for g in range(NG):
                    t = slice(g * GT, (g + 1) * GT)
                    r = prod[layer][:, 0, t, :]
                    step(nc.vector.tensor_tensor(r, wh[layer][:, t, :],
                                                 wts[:, layer, 0, t].unsqueeze(2).broadcast_to((P, GT, E)), ALU.mult))
                    for part in range(PARTS):
                        o = xy[layer][:, t, 0, part, :]
                        if part < PARTS - 1:
                            step(nc.vector.tensor_copy(o, r))
                            step(nc.vector.tensor_tensor(r, r, o, ALU.subtract))
                        else:
                            nc.vector.tensor_copy(o, r).then_inc(x_parts, 1)

            def mask(layer, s, g):
                k = (layer * NS + s) * NG + g
                words = lambda ap: ap.bitcast(U32)
                c = words(neg[:, g % RING, :])
                if layer == 0:
                    dve.wait_ge(loaded[g], 16 * NA * (s + 1))
                    if g != 0 or not isinstance(s, int):
                        dve.wait_ge(turned_ready, s * NG + g)
                    nc.vector.tensor_scalar(
                        narrow[:, :].rearrange("p (b g j) -> p g b j", b=GB, g=GR),
                        stage[:, g, :].rearrange("p (g b j) -> p g b j", g=GR, b=GB),
                        0.0, float(CODE[g // KEEP]), ALU.is_gt, ALU.mult).then_inc(narrowed, 1)
                    dve.wait_ge(narrowed, s * NG + g + 1)
                    dve.wait_ge(products, (k + 1) * RB)
                    a = words(pos[:, g % RING, :])
                    nc.vector.transpose(a, words(narrow[:, :])).then_inc(turned_ready, 1)
                    dve.wait_ge(turned_ready, s * NG + g + 1)
                    dve.wait_ge(signs_ready, k + 1)
                    nc.vector.tensor_tensor(c, c, a, ALU.bitwise_and).then_inc(neg_ready, 1)
                else:
                    a = words(kept_at(s, g))
                    dve.wait_ge(signs_ready, k + 1)
                    nc.vector.scalar_tensor_tensor(c, a, BIT[g // KEEP], c, ALU.bitwise_and, ALU.bitwise_and)\
                      .then_inc(neg_ready, 1)
                    dve.wait_ge(neg_ready, k + 1)
                    nc.vector.scalar_tensor_tensor(words(pos[:, g % RING, :]), a, BIT[g // KEEP], c, ALU.bitwise_and,
                                                   ALU.bitwise_xor).then_inc(pos_ready, 1)

            def read_acc(layer, s):
                for r in range(RB):
                    dve.wait_ge(products, FREE_AT_FIRST + ((layer * NS + s) * NG + NG - 1) * RB + r + 1)
                    nc.vector.tensor_reduce(
                        red[:, r, :, :].rearrange("p c f -> p (c f)").rearrange("p (c f) -> p c f", c=2),
                        acc[:, r, 0:2 * XW].rearrange("p (c k f) -> p c f k", c=2, k=PARTS), AX, ALU.add)\
                      .then_inc(acc_read, 1)

            LINKS = [15, 15]

            def epilogue(layer, s):
                n = [0]

                def link(ins):
                    n[0] += 1
                    ins.then_inc(epi, 1)
                    dve.wait_ge(epi, layer * NS * LINKS[0] + s * LINKS[layer] + n[0])

                col = bass.ds(s * RB, RB)
                wide = lambda ap, f: ap.unsqueeze(2).broadcast_to((P, RB, f))
                V = nc.vector
                rinv, empty, total, mean, var, sd = (small[:, i, :] for i in range(6))
                dve.wait_ge(acc_read, (layer * NS + s) * RB + 2 * RB)
                link(V.tensor_tensor(num[:, :, :], red[:, :, 0, :], wide(ab[:, layer, 0, col], E), ALU.mult))
                link(V.tensor_tensor(red[:, :, 1, :], red[:, :, 1, :], wide(ab[:, layer, 1, col], E), ALU.mult))
                link(V.tensor_tensor(num[:, :, :], num[:, :, :], red[:, :, 1, :], ALU.add))
                link(V.tensor_scalar(empty, num[:, :, D], 0.0, None, ALU.is_equal))
                link(V.tensor_tensor(total, num[:, :, D], empty, ALU.add))
                link(V.reciprocal(rinv, total))
                V.tensor_tensor(ysq[:, :, :], wide(empty, D), meanv[:, layer, :].unsqueeze(1).broadcast_to((P, RB, D)), ALU.mult)
                link(V.tensor_tensor(y[:, :, :], num[:, :, 0:D], wide(rinv, D), ALU.mult))
                link(V.tensor_tensor(y[:, :, :], y[:, :, :], ysq[:, :, :], ALU.add))
                if layer == 1:
                    dve.wait_ge(s_bias, 16)
                    link(V.tensor_tensor(y[:, :, :], y[:, :, :], biasr[:, :].unsqueeze(1).broadcast_to((P, RB, D)), ALU.add))
                if layer == 0:
                    link(V.tensor_tensor(y[:, :, :], y[:, :, :], xn[:, col, :], ALU.add))
                else:
                    link(V.tensor_tensor(y[:, :, :], y[:, :, :], xn[:, col, :], ALU.add))
                link(V.tensor_reduce(mean, y[:, :, :], AX, ALU.add))
                link(V.tensor_scalar(mean, mean, 1.0 / D, None, ALU.mult))
                link(V.tensor_tensor(y[:, :, :], y[:, :, :], wide(mean, D), ALU.subtract))
                link(V.tensor_tensor(ysq[:, :, :], y[:, :, :], y[:, :, :], ALU.mult))
                link(V.tensor_reduce(var, ysq[:, :, :], AX, ALU.add))
                V.tensor_scalar(var, var, 1.0 / D, EPS, ALU.mult, ALU.add).then_inc(var_ready, 1)
                dve.wait_ge(std_ready, layer * NS + s + 1)
                if layer == 0:
                    dve.wait_ge(x1_turned, s + 1)
                    dve.wait_ge(x1_kept, s + 1)
                else:
                    dve.wait_ge(stored, 16 * (s + 1))
                V.tensor_tensor(x1s[:, :, :], y[:, :, :], wide(sd, D), ALU.mult).then_inc([x1_ready, out_ready][layer], 1)
                LINKS_SEEN[layer] = n[0]

            LINKS_SEEN = [0, 0]
            LINKS[0], LINKS[1] = 14, 15
            for layer in range(2):
                tables(layer)
                mask(layer, 0, 0)
                mask(layer, 0, 1)
                with dve.Fori(0, NS - 1) as s:
                    mask(layer, s, 2)
                    mask(layer, s, 3)
                    mask(layer, s + 1, 0)
                    read_acc(layer, s)
                    mask(layer, s + 1, 1)
                    epilogue(layer, s)
                mask(layer, NS - 1, 2)
                mask(layer, NS - 1, 3)
                read_acc(layer, NS - 1)
                epilogue(layer, NS - 1)
            assert LINKS_SEEN == LINKS, LINKS_SEEN

        @block.gpsimd
        def _(pool):
            def inverse_std(layer, s):
                pool.wait_ge(var_ready, layer * NS + s + 1)
                nc.gpsimd.tensor_tensor(small[:, 5, :], small[:, 4, :], minus_half[:, :], ALU.pow).then_inc(std_ready, 1)

            pre = [0]

            def step(ins):
                pre[0] += 1
                ins.then_inc(pool_pre, 1)
                pool.wait_ge(pool_pre, pre[0])

            def split_y(layer):
                pool.wait_ge(weights_ready, layer + 1)
                for g in range(NG):
                    t = slice(g * GT, (g + 1) * GT)
                    r = prod[layer][:, 1, t, :]
                    step(nc.gpsimd.tensor_tensor(r, wh[layer][:, t, :],
                                                 wts[:, layer, 1, t].unsqueeze(2).broadcast_to((P, GT, E)), ALU.mult))
                    for part in range(PARTS):
                        o = xy[layer][:, t, 1, part, :]
                        if part < PARTS - 1:
                            step(nc.gpsimd.tensor_copy(o, r))
                            step(nc.gpsimd.tensor_tensor(r, r, o, ALU.subtract))
                        else:
                            nc.gpsimd.tensor_copy(o, r).then_inc(y_parts, 1)

            def positive(s, g):
                k = s * NG + g
                pool.wait_ge(neg_ready, k + 1)
                pool.sem_inc(pool_turn, 1)
                c = neg[:, g % RING, :].bitcast(U32)
                o = pos[:, g % RING, :].bitcast(U32)
                a = kept_at(s, g).bitcast(U32)
                if g < KEEP:
                    nc.gpsimd.tensor_copy(a, o).then_inc(turned_kept, 1)
                else:
                    nc.gpsimd.tensor_tensor(a, a, o, ALU.add).then_inc(turned_kept, 1)
                pool.wait_ge(turned_kept, k + 1)
                nc.gpsimd.tensor_tensor(o, o, c, ALU.subtract).then_inc(pos_ready, 1)

            pool.sem_inc(x1_kept, 1)
            split_y(0)
            with pool.Fori(0, NS) as s:
                for g in range(NG):
                    positive(s, g)
                inverse_std(0, s)
                pool.wait_ge(x1_ready, s + 1)
                nc.gpsimd.tensor_copy(xn[:, bass.ds(s * RB, RB), :], x1s[:, :, :]).then_inc(x1_kept, 1)
            split_y(1)
            with pool.Fori(0, NS) as s:
                inverse_std(1, s)


_INS = ["x", "adj", "L0_gnn_a", "L1_gnn_weight_w", "L1_gnn_weight_a", "L1_gnn_bias"]


def kernel(**inputs):
    import concourse.bacc as bacc
    from concourse.bass_utils import run_bass_kernel_spmd as run

    nc = bacc.Bacc("TRN2", target_bir_lowering=False, num_devices=1)
    arrays, args = {}, []
    for name in _INS:
        a = np.ascontiguousarray(inputs[name])
        arrays[f"in_{name}"] = a
        args.append(nc.dram_tensor(f"in_{name}", a.shape, mybir.dt.from_np(a.dtype), kind="ExternalInput").ap())
    arrays["identity"] = np.eye(P, dtype=np.float32)
    args.append(nc.dram_tensor("identity", (P, P), F32, kind="ExternalInput").ap())
    out = nc.dram_tensor("out", arrays["in_x"].shape, F32, kind="ExternalOutput").ap()
    gat_kernel(nc, *args, out)
    r = run(nc, [arrays], core_ids=[0])
    return r.results[0]["out"]
```

```python
from contextlib import ExitStack

import numpy as np

import concourse.bass as bass
from concourse import mybir

ALU = mybir.AluOpType
ACT = mybir.ActivationFunctionType
AX = mybir.AxisListType.X
F32 = mybir.dt.float32
BF16 = mybir.dt.bfloat16
FP8 = mybir.dt.float8e4
I8 = mybir.dt.int8
U8 = mybir.dt.uint8
I32 = mybir.dt.int32
U32 = mybir.dt.uint32

P = 128
Q = 32
BYTES = 4
SLOPE = 0.01
EPS = 1e-5


def gat_kernel(nc, x, adj, a0, w1, a1, bias1, ident, out):
    N, D = x.shape
    IB = N // P
    SUP = 512
    NS = N // SUP
    RB = SUP // P
    GR = SUP // Q
    NA = P // Q
    NB = N // NA // P
    TILES = NB * BYTES
    GB = 2
    NG = NB // GB
    GT = GB * BYTES
    GW = GB * GR * Q
    GN = GW * BYTES
    JC = GB * P
    E = D + 1
    PARTS = 3
    XW = PARTS * E
    KEEP = NG // 2
    RING = NG
    SLOTS = 2
    CODE = [0x20, 0x40]
    BIT = [0x20202020, 0x40404040]
    RESCALE = 2.0 ** -4
    FREE_AT_FIRST = RING * RB
    WH_BANK = 7

    ctx = ExitStack()
    with ctx:
        def sb(name, shape, dt):
            return ctx.enter_context(nc.sbuf_tensor(name, shape, dt))

        def sem(name):
            return ctx.enter_context(nc.semaphore(name))

        kept = sb("kept", [P, NS * KEEP * GN], U8)
        stage = sb("stage", [P, SLOTS, GR * JC], I32)
        narrow = sb("narrow", [P, GN], U8)
        turned = sb("turned", [P, SLOTS, GN], U8)
        neg = sb("neg", [P, RING, GN], U8)
        pos = sb("pos", [P, RING, GN], U8)
        xT = sb("xT", [D, N], F32)
        xn = sb("xn", [P, IB, D], F32)
        xy_old = sb("xy_old", [P, TILES * 2 * XW], BF16)
        red = sb("red", [P, RB, 2, E], F32)
        num = sb("num", [P, RB, E], F32)
        y = num[:, :, 0:D]
        ysq = red[:, :, 0, 0:D]
        x1s = sb("x1s", [P, RB, D], F32)
        small = sb("small", [P, 8, RB], F32)
        idf = sb("idf", [P, P], F32)
        onesN = sb("onesN", [P, P], F32)
        one_row = sb("one_row", [1, P], F32)
        minus_half = sb("minus_half", [P, RB], F32)
        acol = sb("acol", [D, 4], F32)
        wext1 = sb("wext1", [D, E], F32)
        wT = sb("wT", [D, D], F32)
        arep = sb("arep", [D, 2, P], F32)
        dcol = sb("dcol", [P, 2, TILES], F32)
        scol = sb("scol", [P, 2, IB], F32)
        mcol = sb("mcol", [P, 8], F32)
        ab = sb("ab", [P, 2, 2, IB], F32)
        wts = sb("wts", [P, 2, 2, TILES], F32)
        meanv = sb("meanv", [P, 2, D], F32)
        hsum = sb("hsum", [P, D], F32)
        arow = sb("arow", [P, 2 * D], F32)
        biasr = sb("biasr", [P, D], F32)

        old_f = xy_old[:, :].bitcast(F32)
        stage_f = stage[:, :, :].rearrange("p s n -> p (s n)").bitcast(F32)
        TAB = TILES * E
        kept_f = kept[:, :].bitcast(F32)
        tail = NS * KEEP * GN // 4
        wh = [kept_f[:, tail - TAB:tail].rearrange("p (t f) -> p t f", f=E),
              old_f[:, 0:TAB].rearrange("p (t f) -> p t f", f=E)]
        prod = [kept_f[:, tail - 3 * TAB:tail - TAB].rearrange("p (c t f) -> p c t f", c=2, f=E),
                old_f[:, TAB:3 * TAB].rearrange("p (c t f) -> p c t f", c=2, f=E)]
        h_raw = kept_f[:, tail - 3 * TAB - TILES * D:tail - 3 * TAB]
        XYW = TILES * 2 * XW // 2
        xy1 = stage_f[:, 0:XYW].bitcast(BF16).rearrange("p (t c k f) -> p t c k f", c=2, k=PARTS, f=E)
        xy = [xy_old[:, :].rearrange("p (t c k f) -> p t c k f", c=2, k=PARTS, f=E), xy1]

        acc = ctx.enter_context(nc.psum_tensor("acc", [P, RB, 512], F32))
        srow = ctx.enter_context(nc.psum_tensor("srow", [P, 2 * 512], F32))
        flip = ctx.enter_context(nc.psum_tensor("flip", [P, 512], F32))
        misc = ctx.enter_context(nc.psum_tensor("misc", [P, 512], F32))

        loaded = [sem(f"loaded{g}") for g in range(SLOTS)]
        s_x = sem("s_x")
        s_h = sem("s_h")
        s_w = sem("s_w")
        s_bias = sem("s_bias")
        const_ready = sem("const_ready")
        w_ready = sem("w_ready")
        xT_psum = sem("xT_psum")
        xT_ready = sem("xT_ready")
        tab_psum = sem("tab_psum")
        tab_ready = sem("tab_ready")
        max_step = sem("max_step")
        max_psum = sem("max_psum")
        shift_ready = sem("shift_ready")
        exp_ready = sem("exp_ready")
        dve_pre = sem("dve_pre")
        pool_pre = sem("pool_pre")
        weights_ready = sem("weights_ready")
        x_parts = sem("x_parts")
        y_parts = sem("y_parts")
        srow_ready = sem("srow_ready")
        narrowed = sem("narrowed")
        turned_ready = sem("turned_ready")
        turned_kept = sem("turned_kept")
        signs_ready = sem("signs_ready")
        neg_ready = sem("neg_ready")
        pos_ready = sem("pos_ready")
        pe_turn = sem("pe_turn")
        act_turn = sem("act_turn")
        pool_turn = sem("pool_turn")
        products = sem("products")
        acc_read = sem("acc_read")
        epi = sem("epi")
        var_ready = sem("var_ready")
        std_ready = sem("std_ready")
        x1_ready = sem("x1_ready")
        x1_turned = sem("x1_turned")
        x1_kept = sem("x1_kept")
        out_ready = sem("out_ready")
        stored = sem("stored")

        block = ctx.enter_context(nc.Block())

        xT_blocks = xT[:, :].rearrange("d (h r a i) -> d h r a i", h=2, r=RB, a=NA)

        def xT_at(s):
            if isinstance(s, int):
                return xT_blocks[:, s % 2, :, s // 2, :]
            return xT_blocks[:, bass.ds(s % 2, 1), :, bass.ds(s // 2, 1), :].rearrange("d h r a i -> d (h r a) i")

        def kept_at(s, g):
            return kept[:, bass.ds(s * (KEEP * GN) + (g % KEEP) * GN, GN)]

        @block.sync
        def _(sp):
            sp.sem_inc(stored, 16)
            sp.dma_start(idf[:, :], ident).then_inc(s_x, 16)
            sp.dma_start(xn[:, :, :], x.rearrange("(b p) d -> p b d", p=P)).then_inc(s_x, 16)
            sp.dma_start(arow[:, :], a0.rearrange("k o -> o k").broadcast_to((P, 2 * D))).then_inc(s_x, 16)
            for a in range(NA):
                sp.dma_start(h_raw[Q * a:Q * a + Q, :].rearrange("t (b e) -> t b e", b=NB),
                             x[a * (N // NA):(a + 1) * (N // NA), :].rearrange("(b t e) d -> t b (e d)", t=Q, e=BYTES))\
                  .then_inc(s_h, 16)
            sp.dma_start(acol[:, 0:1], a0[0:D, :]).then_inc(s_w, 16)
            sp.dma_start(acol[:, 1:2], a0[D:2 * D, :]).then_inc(s_w, 16)
            sp.dma_start(acol[:, 2:3], a1[0:D, :]).then_inc(s_w, 16)
            sp.dma_start(acol[:, 3:4], a1[D:2 * D, :]).then_inc(s_w, 16)
            sp.dma_start(wext1[:, 0:D], w1).then_inc(s_w, 16)
            sp.dma_start(biasr[:, :], bias1.rearrange("(o d) -> o d", o=1).broadcast_to((P, D))).then_inc(s_bias, 16)

            def load(s, g):
                rows = adj[bass.ds(s * SUP, SUP), :].rearrange("(g p) j -> p g j", p=Q)
                for a in range(NA):
                    c = a * (N // NA) + g * JC
                    sp.dma_start(stage[Q * a:Q * a + Q, g % SLOTS, :].rearrange("p (g j) -> p g j", j=JC),
                                 rows[:, :, c:c + JC]).then_inc(loaded[g % SLOTS], 16)

            for g in range(NG):
                if g >= SLOTS:
                    sp.wait_ge(narrowed, g - SLOTS + 1)
                load(0, g)
            with sp.Fori(1, NS) as s:
                for g in range(NG):
                    sp.wait_ge(narrowed, s * NG + g - SLOTS + 1)
                    load(s, g)

            with sp.Fori(0, NS) as s:
                sp.wait_ge(out_ready, s + 1)
                sp.dma_start(out[bass.ds(s * SUP, SUP), :].rearrange("(b p) d -> p b d", p=P),
                             x1s[:, :, :]).then_inc(stored, 16)
            sp.wait_ge(stored, 16 * (NS + 1))

        @block.tensor
        def _(pe):
            pe.sem_inc(x1_turned, 1)
            pe.sem_inc(products, FREE_AT_FIRST)
            pe.wait_ge(s_x, 48)
            pe.wait_ge(s_w, 80)
            nc.tensor.transpose(misc[0:D, 0:D], wext1[:, 0:D], idf[0:D, 0:D]).then_inc(max_psum, 1)
            pe.wait_ge(w_ready, 1)
            nc.tensor.matmul(misc[0:D, 64:66], wT[:, :], acol[:, 2:4], start=True, stop=True).then_inc(max_psum, 1)
            def turn_x(t):
                if t >= RB:
                    pe.wait_ge(xT_ready, t - RB + 1)
                for b in range(RB):
                    last = nc.tensor.transpose(acc[0:D, t % RB, b * P:(b + 1) * P], xn[:, t * RB + b, :], idf[:, :])
                last.then_inc(xT_psum, 1)

            def score_row(layer, s):
                nc.tensor.matmul(srow[:, bass.ds((s % 2) * 512, 512)], arep[:, layer, :], xT_at(s),
                                 start=True, stop=True).then_inc(srow_ready, 1)

            def shift(layer):
                pe.wait_ge(max_step, 3 * layer + 1)
                nc.tensor.transpose(flip[0:1, 128:256], mcol[:, 0:1], idf[:, :]).then_inc(max_psum, 1)
                pe.wait_ge(max_step, 3 * layer + 2)
                nc.tensor.matmul(srow[:, 512:512 + D], onesN[:, :], hsum[:, :], start=True, stop=True).then_inc(max_psum, 1)
                pe.wait_ge(max_step, 3 * layer + 3)
                nc.tensor.matmul(flip[:, 256:257], one_row[:, :], mcol[0:1, 1:2], start=True, stop=True).then_inc(max_psum, 1)

            def tables0():
                for t in range(2):
                    turn_x(t)
                pe.wait_ge(w_ready, 3)
                pe.wait_ge(xT_ready, 1)
                score_row(0, 0)
                shift(0)
                for t in range(2, NS):
                    turn_x(t)
                pe.wait_ge(xT_ready, NS)

            def tables1():
                pe.wait_ge(xT_ready, 2 * NS)
                pe.wait_ge(acc_read, NS * RB + RB)
                xcols = xT[:, :].rearrange("d (b c e) -> d b e c", b=NB, e=BYTES)
                for t in range(TILES):
                    b = t // WH_BANK
                    dst = acc[:, b, :] if b < RB else misc[:, :]
                    c = (t % WH_BANK) * E
                    last = nc.tensor.matmul(dst[:, c:c + E], xcols[:, t // BYTES, t % BYTES], wext1[:, :],
                                            start=True, stop=True)
                    if t % WH_BANK == WH_BANK - 1 or t == TILES - 1:
                        last.then_inc(tab_psum, 1)
                score_row(1, 0)
                shift(1)
                pe.wait_ge(tab_ready, RB + 1)
                for b in range(IB):
                    last = nc.tensor.matmul(misc[:, b:b + 1], xT_at(b // RB)[:, b % RB, :], arep[:, 1, 0:1],
                                            start=True, stop=True)
                last.then_inc(tab_psum, 1)

            def granule(layer, s, g):
                k = (layer * NS + s) * NG + g
                pe.wait_ge(neg_ready, k + 1)
                pe.wait_ge(pos_ready, k + 1)
                pe.sem_inc(pe_turn, 1)
                pe.wait_ge(x_parts, layer * NG + g + 1)
                pe.wait_ge(y_parts, layer * NG + g + 1)
                masks = [m[:, g, :].bitcast(FP8).rearrange("p (b i e) -> p b e i", b=GB, e=BYTES) for m in (pos, neg)]
                for r in range(RB):
                    if g == 0:
                        pe.wait_ge(acc_read, (layer * NS + s) * RB + r + 1)
                    if g == 0:
                        pe.sem_inc(pe_turn, 1)
                    for t in range(GT):
                        for c in range(2):
                            last = nc.tensor.matmul(
                                acc[:, r, c * XW:(c + 1) * XW], masks[c][:, t // BYTES, t % BYTES, r * P:(r + 1) * P],
                                xy[layer][:, g * GT + t, c].rearrange("p k f -> p (k f)"),
                                start=(g == 0 and t == 0 and c == 0), stop=(g == NG - 1 and t == GT - 1),
                                skip_group_check=True)
                    last.then_inc(products, 1)

            def turn_x1(s):
                pe.wait_ge(x1_ready, s + 1)
                pe.wait_ge(xT_ready, NS + s)
                pe.sem_inc(pe_turn, 1)
                for b in range(RB):
                    last = nc.tensor.transpose(flip[0:D, b * P:(b + 1) * P], x1s[:, b, :], idf[:, :])
                last.then_inc(x1_turned, 1)

            for layer in range(2):
                [tables0, tables1][layer]()
                granule(layer, 0, 0)
                granule(layer, 0, 1)
                with pe.Fori(0, NS - 1) as s:
                    score_row(layer, s + 1)
                    granule(layer, s, 2)
                    granule(layer, s, 3)
                    granule(layer, s + 1, 0)
                    granule(layer, s + 1, 1)
                    if layer == 0:
                        turn_x1(s)
                granule(layer, NS - 1, 2)
                granule(layer, NS - 1, 3)
                if layer == 0:
                    turn_x1(NS - 1)

        @block.scalar
        def _(act):
            act.wait_ge(max_psum, 1)
            nc.scalar.copy(wT[:, :], misc[0:D, 0:D]).then_inc(w_ready, 1)
            def tables0():
                for t in range(NS):
                    if t == 2:
                        exps(0)
                    act.wait_ge(xT_psum, t + 1)
                    nc.scalar.copy(xT_at(t), acc[0:D, t % RB, :].rearrange("d (r i) -> d r i", r=RB)).then_inc(xT_ready, 1)

            def tables1():
                for b in range(RB + 1):
                    t0, t1 = b * WH_BANK, min((b + 1) * WH_BANK, TILES)
                    src = acc[:, b, 0:(t1 - t0) * E] if b < RB else misc[:, 0:(t1 - t0) * E]
                    act.wait_ge(tab_psum, b + 1)
                    nc.scalar.copy(wh[1][:, t0:t1, :].rearrange("p t f -> p (t f)"), src).then_inc(tab_ready, 1)
                exps(1)
                act.wait_ge(tab_psum, RB + 2)
                nc.scalar.copy(scol[:, 1, :], misc[:, 0:IB]).then_inc(tab_ready, 1)

            def exps(layer):
                act.wait_ge(shift_ready, 2 * layer + 1)
                nc.scalar.activation(wts[:, layer, 0, :], dcol[:, layer, :], ACT.Exp, bias=mcol[:, 2:3]).then_inc(exp_ready, 1)
                nc.scalar.activation(wts[:, layer, 1, :], dcol[:, layer, :], ACT.Exp, bias=mcol[:, 3:4],
                                     scale=SLOPE).then_inc(exp_ready, 1)

            def row_factors(layer):
                act.wait_ge(shift_ready, 2 * layer + 2)
                nc.scalar.activation(ab[:, layer, :, :], ab[:, layer, :, :], ACT.Exp).then_inc(exp_ready, 1)

            def signs(layer, s, g):
                k = (layer * NS + s) * NG + g
                if g == 0:
                    act.wait_ge(srow_ready, layer * NS + s + 1)
                act.wait_ge(products, (k + 1) * RB)
                act.sem_inc(act_turn, 1)
                o = neg[:, g, :].bitcast(I8).rearrange("p (b i e) -> p b e i", b=GB, e=BYTES)
                for t in range(GT):
                    col = g * GT + t
                    last = nc.scalar.activation(o[:, t // BYTES, t % BYTES, :], srow[:, bass.ds((s % 2) * 512, 512)],
                                                ACT.Sign, bias=dcol[:, layer, col:col + 1])
                last.then_inc(signs_ready, 1)

            def copy_x1(s):
                act.wait_ge(x1_turned, s + 2)
                act.sem_inc(act_turn, 1)
                nc.scalar.copy(xT_at(s), flip[0:D, :].rearrange("d (r i) -> d r i", r=RB)).then_inc(xT_ready, 1)

            for layer in range(2):
                [tables0, tables1][layer]()
                for g in range(NG):
                    signs(layer, 0, g)
                row_factors(layer)
                with act.Fori(0, NS - 1) as s:
                    for g in range(NG):
                        signs(layer, s + 1, g)
                    if layer == 0:
                        copy_x1(s)
                if layer == 0:
                    copy_x1(NS - 1)

        @block.vector
        def _(dve):
            dve.sem_inc(acc_read, RB)
            pre = [0]

            def step(ins):
                pre[0] += 1
                ins.then_inc(dve_pre, 1)
                dve.wait_ge(dve_pre, pre[0])

            nc.vector.memset(onesN[:, :], 1.0 / N).then_inc(const_ready, 1)
            nc.vector.memset(one_row[:, :], 1.0).then_inc(const_ready, 1)
            nc.vector.memset(minus_half[:, :], -0.5).then_inc(const_ready, 1)
            dve.wait_ge(s_x, 48)
            dve.wait_ge(s_w, 80)
            nc.vector.tensor_copy(arep[:, 0, :], acol[:, 0:1].broadcast_to((D, P)))
            dve.wait_ge(max_psum, 2)
            nc.vector.tensor_copy(arep[:, 1, :], misc[0:D, 64:65].broadcast_to((D, P))).then_inc(w_ready, 1)
            nc.vector.tensor_copy(wext1[:, D:E], misc[0:D, 65:66]).then_inc(w_ready, 1)

            def scores0():
                h = h_raw.rearrange("p (t d) -> p t d", d=D)
                for col, table, half in ((dcol[:, 0, :], h, 1), (scol[:, 0, :], xn[:, :, :], 0)):
                    if half:
                        dve.wait_ge(s_h, 16 * NA)
                        nc.vector.tensor_copy(wh[0][:, :, 0:D], h)
                    t = prod[0][:, half, :, 0:D]
                    a = arow[:, half * D:(half + 1) * D].unsqueeze(1).broadcast_to((P, TILES, D))
                    step(nc.vector.tensor_tensor(t, table, a, ALU.mult))
                    step(nc.vector.tensor_reduce(col, t, AX, ALU.add))

            def tables(layer):
                w = wh[layer]
                if layer == 0:
                    scores0()
                else:
                    dve.wait_ge(tab_ready, RB + 1)
                    step(nc.vector.tensor_copy(dcol[:, layer, :], w[:, :, D]))
                nc.vector.tensor_reduce(mcol[:, 0:1], dcol[:, layer, :], AX, ALU.max).then_inc(max_step, 1)
                nc.vector.tensor_reduce(hsum[:, :], w[:, :, 0:D].rearrange("p t f -> p f t"), AX, ALU.add).then_inc(max_step, 1)
                step(nc.vector.memset(w[:, :, D:E], 1.0))
                dve.wait_ge(max_psum, 3 + 3 * layer)
                nc.vector.tensor_reduce(mcol[0:1, 1:2], flip[0:1, 128:256], AX, ALU.max).then_inc(max_step, 1)
                dve.wait_ge(max_psum, 5 + 3 * layer)
                nc.vector.tensor_copy(meanv[:, layer, :], srow[:, 512:512 + D])
                step(nc.vector.tensor_scalar(mcol[:, 2:3], flip[:, 256:257], -1.0, None, ALU.mult))
                nc.vector.tensor_scalar(mcol[:, 3:4], mcol[:, 2:3], SLOPE, None, ALU.mult).then_inc(shift_ready, 1)
                dve.wait_ge(exp_ready, 3 * layer + 2)
                h = KEEP * GT
                nc.vector.tensor_scalar(wts[:, layer, :, h:TILES], wts[:, layer, :, h:TILES], RESCALE, None, ALU.mult)\
                  .then_inc(weights_ready, 1)
                dve.wait_ge(weights_ready, layer + 1)

            def row_factors(layer):
                if layer:
                    dve.wait_ge(tab_ready, RB + 2)
                step(nc.vector.tensor_scalar(scol[:, layer, :], scol[:, layer, :], mcol[:, 2:3], None, ALU.subtract))
                nc.vector.tensor_scalar(ab[:, layer, 0, :], scol[:, layer, :], 1 - SLOPE, 0.0, ALU.mult, ALU.min)
                nc.vector.tensor_scalar(ab[:, layer, 1, :], scol[:, layer, :], SLOPE - 1, 0.0, ALU.mult, ALU.min)\
                  .then_inc(shift_ready, 1)

            def split_x(layer, g):
                t = slice(g * GT, (g + 1) * GT)
                r = prod[layer][:, 0, t, :]
                step(nc.vector.tensor_tensor(r, wh[layer][:, t, :],
                                             wts[:, layer, 0, t].unsqueeze(2).broadcast_to((P, GT, E)), ALU.mult))
                for part in range(PARTS):
                    o = xy[layer][:, t, 0, part, :]
                    if part < PARTS - 1:
                        step(nc.vector.tensor_copy(o, r))
                        step(nc.vector.tensor_tensor(r, r, o, ALU.subtract))
                    else:
                        nc.vector.tensor_copy(o, r).then_inc(x_parts, 1)

            def words(ap):
                return ap.bitcast(U32)

            def turn(s, g):
                k = s * NG + g
                dve.wait_ge(loaded[g % SLOTS], 16 * NA * (s * (NG // SLOTS) + g // SLOTS + 1))
                if g != 0 or not isinstance(s, int):
                    dve.wait_ge(turned_ready, k)
                nc.vector.tensor_scalar(
                    narrow[:, :].rearrange("p (b g j) -> p g b j", b=GB, g=GR),
                    stage[:, g % SLOTS, :].rearrange("p (g b j) -> p g b j", g=GR, b=GB),
                    0.0, float(CODE[g // KEEP]), ALU.is_gt, ALU.mult).then_inc(narrowed, 1)
                dve.wait_ge(turned_kept, k + 1)
                dve.wait_ge(narrowed, k + 1)
                nc.vector.transpose(words(turned[:, g % SLOTS, :]), words(narrow[:, :])).then_inc(turned_ready, 1)

            def mask(layer, s, g):
                k = (layer * NS + s) * NG + g
                c = words(neg[:, g, :])
                dve.wait_ge(signs_ready, k + 1)
                if layer == 0:
                    dve.wait_ge(turned_ready, s * NG + g + 1)
                    a = words(turned[:, g % SLOTS, :])
                    nc.vector.tensor_tensor(c, c, a, ALU.bitwise_and).then_inc(neg_ready, 1)
                    dve.wait_ge(neg_ready, k + 1)
                    nc.vector.tensor_tensor(words(pos[:, g, :]), a, c, ALU.bitwise_xor).then_inc(pos_ready, 1)
                else:
                    dve.wait_ge(turned_kept, NS * NG + SLOTS)
                    a = words(kept_at(s, g))
                    nc.vector.scalar_tensor_tensor(c, a, BIT[g // KEEP], c, ALU.bitwise_and, ALU.bitwise_and)\
                      .then_inc(neg_ready, 1)
                    dve.wait_ge(neg_ready, k + 1)
                    nc.vector.scalar_tensor_tensor(words(pos[:, g, :]), a, BIT[g // KEEP], c, ALU.bitwise_and,
                                                   ALU.bitwise_xor).then_inc(pos_ready, 1)

            def read_acc(layer, s):
                for r in range(RB):
                    dve.wait_ge(products, FREE_AT_FIRST + ((layer * NS + s) * NG + NG - 1) * RB + r + 1)
                    nc.vector.tensor_reduce(
                        red[:, r, :, :].rearrange("p c f -> p (c f)").rearrange("p (c f) -> p c f", c=2),
                        acc[:, r, 0:2 * XW].rearrange("p (c k f) -> p c f k", c=2, k=PARTS), AX, ALU.add)\
                      .then_inc(acc_read, 1)

            LINKS = [15, 15]

            def epilogue(layer, s):
                n = [0]

                def link(ins):
                    n[0] += 1
                    ins.then_inc(epi, 1)
                    dve.wait_ge(epi, layer * NS * LINKS[0] + s * LINKS[layer] + n[0])

                col = bass.ds(s * RB, RB)
                wide = lambda ap, f: ap.unsqueeze(2).broadcast_to((P, RB, f))
                V = nc.vector
                rinv, empty, total, mean, var, sd = (small[:, i, :] for i in range(6))
                dve.wait_ge(acc_read, (layer * NS + s) * RB + 2 * RB)
                dve.wait_ge(exp_ready, 3 * (layer + 1))
                link(V.tensor_tensor(num[:, :, :], red[:, :, 0, :], wide(ab[:, layer, 0, col], E), ALU.mult))
                link(V.tensor_tensor(red[:, :, 1, :], red[:, :, 1, :], wide(ab[:, layer, 1, col], E), ALU.mult))
                link(V.tensor_tensor(num[:, :, :], num[:, :, :], red[:, :, 1, :], ALU.add))
                link(V.tensor_scalar(empty, num[:, :, D], 0.0, None, ALU.is_equal))
                link(V.tensor_tensor(total, num[:, :, D], empty, ALU.add))
                link(V.reciprocal(rinv, total))
                V.tensor_tensor(ysq[:, :, :], wide(empty, D), meanv[:, layer, :].unsqueeze(1).broadcast_to((P, RB, D)), ALU.mult)
                link(V.tensor_tensor(y[:, :, :], num[:, :, 0:D], wide(rinv, D), ALU.mult))
                link(V.tensor_tensor(y[:, :, :], y[:, :, :], ysq[:, :, :], ALU.add))
                if layer == 1:
                    dve.wait_ge(s_bias, 16)
                    link(V.tensor_tensor(y[:, :, :], y[:, :, :], biasr[:, :].unsqueeze(1).broadcast_to((P, RB, D)), ALU.add))
                if layer == 0:
                    link(V.tensor_tensor(y[:, :, :], y[:, :, :], xn[:, col, :], ALU.add))
                else:
                    link(V.tensor_tensor(y[:, :, :], y[:, :, :], xn[:, col, :], ALU.add))
                link(V.tensor_reduce(mean, y[:, :, :], AX, ALU.add))
                link(V.tensor_scalar(mean, mean, 1.0 / D, None, ALU.mult))
                link(V.tensor_tensor(y[:, :, :], y[:, :, :], wide(mean, D), ALU.subtract))
                link(V.tensor_tensor(ysq[:, :, :], y[:, :, :], y[:, :, :], ALU.mult))
                link(V.tensor_reduce(var, ysq[:, :, :], AX, ALU.add))
                V.tensor_scalar(var, var, 1.0 / D, EPS, ALU.mult, ALU.add).then_inc(var_ready, 1)
                dve.wait_ge(std_ready, layer * NS + s + 1)
                if layer == 0:
                    dve.wait_ge(x1_turned, s + 1)
                    dve.wait_ge(x1_kept, s + 1)
                else:
                    dve.wait_ge(stored, 16 * (s + 1))
                V.tensor_tensor(x1s[:, :, :], y[:, :, :], wide(sd, D), ALU.mult).then_inc([x1_ready, out_ready][layer], 1)
                LINKS_SEEN[layer] = n[0]

            LINKS_SEEN = [0, 0]
            LINKS[0], LINKS[1] = 14, 15
            turn(0, 0)
            turn(0, 1)
            for layer in range(2):
                tables(layer)
                split_x(layer, 0)
                mask(layer, 0, 0)
                if layer == 0:
                    turn(0, 2)
                split_x(layer, 1)
                mask(layer, 0, 1)
                split_x(layer, 2)
                split_x(layer, 3)
                row_factors(layer)
                with dve.Fori(0, NS - 1) as s:
                    if layer == 0:
                        turn(s, 3)
                    mask(layer, s, 2)
                    if layer == 0:
                        turn(s + 1, 0)
                    mask(layer, s, 3)
                    if layer == 0:
                        turn(s + 1, 1)
                    mask(layer, s + 1, 0)
                    read_acc(layer, s)
                    if layer == 0:
                        turn(s + 1, 2)
                    mask(layer, s + 1, 1)
                    epilogue(layer, s)
                if layer == 0:
                    turn(NS - 1, 3)
                mask(layer, NS - 1, 2)
                mask(layer, NS - 1, 3)
                read_acc(layer, NS - 1)
                epilogue(layer, NS - 1)
            assert LINKS_SEEN == LINKS, LINKS_SEEN

        @block.gpsimd
        def _(pool):
            def inverse_std(layer, s):
                pool.wait_ge(var_ready, layer * NS + s + 1)
                nc.gpsimd.tensor_tensor(small[:, 5, :], small[:, 4, :], minus_half[:, :], ALU.pow).then_inc(std_ready, 1)

            pre = [0]

            def step(ins):
                pre[0] += 1
                ins.then_inc(pool_pre, 1)
                pool.wait_ge(pool_pre, pre[0])

            def split_y(layer, g):
                t = slice(g * GT, (g + 1) * GT)
                r = prod[layer][:, 1, t, :]
                step(nc.gpsimd.tensor_tensor(r, wh[layer][:, t, :],
                                             wts[:, layer, 1, t].unsqueeze(2).broadcast_to((P, GT, E)), ALU.mult))
                for part in range(PARTS):
                    o = xy[layer][:, t, 1, part, :]
                    if part < PARTS - 1:
                        step(nc.gpsimd.tensor_copy(o, r))
                        step(nc.gpsimd.tensor_tensor(r, r, o, ALU.subtract))
                    else:
                        nc.gpsimd.tensor_copy(o, r).then_inc(y_parts, 1)

            def keep(s, g):
                pool.wait_ge(turned_ready, s * NG + g + 1)
                if g >= KEEP:
                    pool.wait_ge(turned_kept, s * NG + g - KEEP + 1 + SLOTS)
                pool.sem_inc(pool_turn, 1)
                a = kept_at(s, g).bitcast(U32)
                t = turned[:, g % SLOTS, :].bitcast(U32)
                if g < KEEP:
                    nc.gpsimd.tensor_copy(a, t).then_inc(turned_kept, 1)
                else:
                    nc.gpsimd.tensor_tensor(a, a, t, ALU.add).then_inc(turned_kept, 1)

            pool.sem_inc(turned_kept, SLOTS)
            pool.sem_inc(x1_kept, 1)

            def residual(s):
                inverse_std(0, s)
                pool.wait_ge(x1_ready, s + 1)
                nc.gpsimd.tensor_copy(xn[:, bass.ds(s * RB, RB), :], x1s[:, :, :]).then_inc(x1_kept, 1)

            pool.wait_ge(weights_ready, 1)
            for g in range(NG):
                split_y(0, g)
                if g < NG - 1:
                    keep(0, g)
            with pool.Fori(0, NS - 1) as s:
                keep(s, NG - 1)
                for g in range(NG - 1):
                    keep(s + 1, g)
                residual(s)
            keep(NS - 1, NG - 1)
            residual(NS - 1)
            pool.wait_ge(weights_ready, 2)
            for g in range(NG):
                split_y(1, g)
            with pool.Fori(0, NS) as s:
                inverse_std(1, s)


_INS = ["x", "adj", "L0_gnn_a", "L1_gnn_weight_w", "L1_gnn_weight_a", "L1_gnn_bias"]


def kernel(**inputs):
    import concourse.bacc as bacc
    from concourse.bass_utils import run_bass_kernel_spmd as run

    nc = bacc.Bacc("TRN2", target_bir_lowering=False, num_devices=1)
    arrays, args = {}, []
    for name in _INS:
        a = np.ascontiguousarray(inputs[name])
        arrays[f"in_{name}"] = a
        args.append(nc.dram_tensor(f"in_{name}", a.shape, mybir.dt.from_np(a.dtype), kind="ExternalInput").ap())
    arrays["identity"] = np.eye(P, dtype=np.float32)
    args.append(nc.dram_tensor("identity", (P, P), F32, kind="ExternalInput").ap())
    out = nc.dram_tensor("out", arrays["in_x"].shape, F32, kind="ExternalOutput").ap()
    gat_kernel(nc, *args, out)
    r = run(nc, [arrays], core_ids=[0])
    return r.results[0]["out"]
```

```python
from contextlib import ExitStack

import numpy as np

import concourse.bass as bass
from concourse import mybir

ALU = mybir.AluOpType
ACT = mybir.ActivationFunctionType
AX = mybir.AxisListType.X
F32 = mybir.dt.float32
BF16 = mybir.dt.bfloat16
FP8 = mybir.dt.float8e4
I8 = mybir.dt.int8
U8 = mybir.dt.uint8
I32 = mybir.dt.int32
U32 = mybir.dt.uint32

P = 128
Q = 32
BYTES = 4
SLOPE = 0.01
EPS = 1e-5


def gat_kernel(nc, x, adj, a0, w1, a1, bias1, ident, out):
    N, D = x.shape
    IB = N // P
    SUP = 512
    NS = N // SUP
    RB = SUP // P
    GR = SUP // Q
    NA = P // Q
    NB = N // NA // P
    TILES = NB * BYTES
    GB = 2
    NG = NB // GB
    GT = GB * BYTES
    GW = GB * GR * Q
    GN = GW * BYTES
    JC = GB * P
    E = D + 1
    PARTS = 3
    XW = PARTS * E
    KEEP = NG // 2
    RING = NG
    SLOTS = 2
    CODE = [0x20, 0x40]
    BIT = [0x20202020, 0x40404040]
    RESCALE = 2.0 ** -4
    FREE_AT_FIRST = RING * RB
    WH_BANK = 7

    ctx = ExitStack()
    with ctx:
        def sb(name, shape, dt):
            return ctx.enter_context(nc.sbuf_tensor(name, shape, dt))

        def sem(name):
            return ctx.enter_context(nc.semaphore(name))

        kept = sb("kept", [P, NS * KEEP * GN], U8)
        stage = sb("stage", [P, SLOTS, GR * JC], I32)
        narrow = sb("narrow", [P, GN], U8)
        turned = sb("turned", [P, NG, GN], U8)
        neg = sb("neg", [P, RING, GN], U8)
        pos = sb("pos", [P, RING, GN], U8)
        xT = sb("xT", [D, N], F32)
        xn = sb("xn", [P, IB, D], F32)
        xy_old = sb("xy_old", [P, TILES * 2 * XW], BF16)
        red = sb("red", [P, RB, 2, E], F32)
        num = sb("num", [P, RB, E], F32)
        y = num[:, :, 0:D]
        base = red[:, :, 0, 0:D]
        x1s = sb("x1s", [P, RB, D], F32)
        small = sb("small", [P, 7, RB], F32)
        rden, empty, total, var, minus_mean, rstd, shift_n = (small[:, i, :] for i in range(7))
        LINKS = 8
        bn = sb("bn", [P, RB, 6], F32)
        mv = sb("mv", [P, RB, 2], F32)
        idf = sb("idf", [P, P], F32)
        onesN = sb("onesN", [P, P], F32)
        one_row = sb("one_row", [1, P], F32)
        minus_half = sb("minus_half", [P, RB], F32)
        acol = sb("acol", [D, 3], F32)
        wext1 = sb("wext1", [D, E], F32)
        wT = sb("wT", [D, D], F32)
        arep = sb("arep", [D, 2, P], F32)
        dcol = sb("dcol", [P, 2, TILES], F32)
        scol = sb("scol", [P, 2, IB], F32)
        mcol = sb("mcol", [P, 8], F32)
        ab = sb("ab", [P, 2, 2, IB], F32)
        wts = sb("wts", [P, 2, 2, TILES], F32)
        meanv = sb("meanv", [P, 2, D], F32)
        hsum = sb("hsum", [P, D], F32)
        arow = sb("arow", [P, 3 * D], F32)
        biasr = sb("biasr", [P, D], F32)

        old_f = xy_old[:, :].bitcast(F32)
        stage_f = stage[:, :, :].rearrange("p s n -> p (s n)").bitcast(F32)
        TAB = TILES * E
        kept_f = kept[:, :].bitcast(F32)
        tail = NS * KEEP * GN // 4
        wh = [kept_f[:, tail - TAB:tail].rearrange("p (t f) -> p t f", f=E),
              old_f[:, 0:TAB].rearrange("p (t f) -> p t f", f=E)]
        prod = [kept_f[:, tail - 3 * TAB:tail - TAB].rearrange("p (c t f) -> p c t f", c=2, f=E),
                old_f[:, TAB:3 * TAB].rearrange("p (c t f) -> p c t f", c=2, f=E)]
        h_raw = kept_f[:, tail - 3 * TAB - TILES * D:tail - 3 * TAB]
        XYW = TILES * 2 * XW // 2
        xy1 = stage_f[:, 0:XYW].bitcast(BF16).rearrange("p (t c k f) -> p t c k f", c=2, k=PARTS, f=E)
        xy = [xy_old[:, :].rearrange("p (t c k f) -> p t c k f", c=2, k=PARTS, f=E), xy1]

        s_terms = pos[:, 2:4, :].bitcast(F32).rearrange("p s (b d) -> p (s b) d", d=D)

        acc = ctx.enter_context(nc.psum_tensor("acc", [P, RB, 512], F32))
        srow = ctx.enter_context(nc.psum_tensor("srow", [P, 2 * 512], F32))
        flip = ctx.enter_context(nc.psum_tensor("flip", [P, 512], F32))
        misc = ctx.enter_context(nc.psum_tensor("misc", [P, 512], F32))

        loaded = [sem(f"loaded{g}") for g in range(SLOTS)]
        s_x = sem("s_x")
        s_h = sem("s_h")
        s_a = sem("s_a")
        s_prod = sem("s_prod")
        s_w = sem("s_w")
        h_copied = sem("h_copied")
        arep_ready = sem("arep_ready")
        s_bias = sem("s_bias")
        const_ready = sem("const_ready")
        w_ready = sem("w_ready")
        xT_psum = sem("xT_psum")
        xT_ready = sem("xT_ready")
        tab_psum = sem("tab_psum")
        tab_ready = sem("tab_ready")
        max_step = sem("max_step")
        max_psum = sem("max_psum")
        shift_ready = sem("shift_ready")
        exp_ready = sem("exp_ready")
        dve_pre = sem("dve_pre")
        pool_pre = sem("pool_pre")
        weights_ready = sem("weights_ready")
        x_parts = sem("x_parts")
        y_parts = sem("y_parts")
        srow_ready = sem("srow_ready")
        narrowed = sem("narrowed")
        turned_ready = sem("turned_ready")
        turned_kept = sem("turned_kept")
        signs_ready = sem("signs_ready")
        neg_ready = sem("neg_ready")
        pos_ready = sem("pos_ready")
        pe_turn = sem("pe_turn")
        act_turn = sem("act_turn")
        dve_turn = sem("dve_turn")
        pool_turn = sem("pool_turn")
        products = sem("products")
        acc_read = sem("acc_read")
        epi = sem("epi")
        base_step = sem("base_step")
        base_ready = sem("base_ready")
        var_ready = sem("var_ready")
        std_ready = sem("std_ready")
        x1_ready = sem("x1_ready")
        x1_turned = sem("x1_turned")
        x1_kept = sem("x1_kept")
        stored = sem("stored")

        block = ctx.enter_context(nc.Block())

        xT_blocks = xT[:, :].rearrange("d (h r a i) -> d h r a i", h=2, r=RB, a=NA)

        def xT_at(s):
            if isinstance(s, int):
                return xT_blocks[:, s % 2, :, s // 2, :]
            return xT_blocks[:, bass.ds(s % 2, 1), :, bass.ds(s // 2, 1), :].rearrange("d h r a i -> d (h r a) i")

        def kept_at(s, g):
            return kept[:, bass.ds(s * (KEEP * GN) + (g % KEEP) * GN, GN)]

        @block.sync
        def _(sp):
            sp.sem_inc(stored, 16)
            for a in range(NA):
                sp.dma_start(h_raw[Q * a:Q * a + Q, :].rearrange("t (b e) -> t b e", b=NB),
                             x[a * (N // NA):(a + 1) * (N // NA), :].rearrange("(b t e) d -> t b (e d)", t=Q, e=BYTES))\
                  .then_inc(s_h, 16)
            sp.dma_start(arow[:, 0:2 * D], a0.rearrange("k o -> o k").broadcast_to((P, 2 * D))).then_inc(s_h, 16)
            sp.dma_start(idf[:, :], ident).then_inc(s_a, 16)
            sp.dma_start(acol[:, 0:1], a0[0:D, :]).then_inc(s_a, 16)
            sp.dma_start(xn[:, :, :], x.rearrange("(b p) d -> p b d", p=P)).then_inc(s_x, 16)
            sp.dma_start(acol[:, 1:2], a1[0:D, :]).then_inc(s_w, 16)
            sp.dma_start(acol[:, 2:3], a1[D:2 * D, :]).then_inc(s_w, 16)
            sp.dma_start(wext1[:, 0:D], w1).then_inc(s_w, 16)
            sp.dma_start(biasr[:, :], bias1.rearrange("(o d) -> o d", o=1).broadcast_to((P, D))).then_inc(s_bias, 16)

            def load(s, g):
                rows = adj[bass.ds(s * SUP, SUP), :].rearrange("(g p) j -> p g j", p=Q)
                for a in range(NA):
                    c = a * (N // NA) + g * JC
                    sp.dma_start(stage[Q * a:Q * a + Q, g % SLOTS, :].rearrange("p (g j) -> p g j", j=JC),
                                 rows[:, :, c:c + JC]).then_inc(loaded[g % SLOTS], 16)

            for g in range(NG):
                if g >= SLOTS:
                    sp.wait_ge(narrowed, g - SLOTS + 1)
                load(0, g)
            with sp.Fori(1, NS) as s:
                for g in range(NG):
                    sp.wait_ge(narrowed, s * NG + g - SLOTS + 1)
                    load(s, g)

            with sp.Fori(0, NS) as s:
                sp.wait_ge(x1_ready, NS + s + 2)
                sp.dma_start(out[bass.ds(s * SUP, SUP), :].rearrange("(b p) d -> p b d", p=P),
                             x1s[:, :, :]).then_inc(stored, 16)
            sp.wait_ge(stored, 16 * (NS + 1))

        @block.tensor
        def _(pe):
            pe.sem_inc(x1_turned, 1)
            pe.sem_inc(products, FREE_AT_FIRST)

            def source_vectors():
                pe.wait_ge(s_w, 48)
                nc.tensor.transpose(misc[0:D, 0:D], wext1[:, 0:D], idf[0:D, 0:D]).then_inc(max_psum, 1)
                pe.wait_ge(w_ready, 1)
                nc.tensor.matmul(misc[0:D, 64:66], wT[:, :], acol[:, 1:3], start=True, stop=True).then_inc(max_psum, 1)
                pe.wait_ge(w_ready, 3)
                nc.tensor.matmul(misc[:, 128:128 + D], arep[:, 1, :], idf[0:D, 0:D], start=True, stop=True)\
                  .then_inc(max_psum, 1)

            def turn_x(t):
                if t >= RB:
                    pe.wait_ge(xT_ready, t - RB + 1)
                for b in range(RB):
                    last = nc.tensor.transpose(acc[0:D, t % RB, b * P:(b + 1) * P], xn[:, t * RB + b, :], idf[:, :])
                last.then_inc(xT_psum, 1)

            def score_row(layer, s):
                nc.tensor.matmul(srow[:, bass.ds((s % 2) * 512, 512)], arep[:, layer, :], xT_at(s),
                                 start=True, stop=True).then_inc(srow_ready, 1)

            def shift(layer):
                pe.wait_ge(max_step, 2 * layer + 1)
                nc.tensor.transpose(flip[0:1, 128:256], mcol[:, 0:1], idf[:, :]).then_inc(max_psum, 1)
                pe.wait_ge(max_step, 2 * layer + 2)
                nc.tensor.matmul(flip[:, 256:257], one_row[:, :], mcol[0:1, 1:2], start=True, stop=True).then_inc(max_psum, 1)

            def mean(layer):
                if layer == 0:
                    w = SUP // D
                    pe.wait_ge(w_ready, 4)
                    for b in range(0, IB, w):
                        last = nc.tensor.matmul(misc[:, :], onesN[:, :], xn[:, b:b + w, :].rearrange("p b d -> p (b d)"),
                                                start=b == 0, stop=b == IB - w)
                else:
                    pe.wait_ge(max_step, 5)
                    last = nc.tensor.matmul(misc[:, 448:448 + D], onesN[:, :], hsum[:, :], start=True, stop=True)
                last.then_inc(max_psum, 1)

            def tables0():
                pe.wait_ge(const_ready, 3)
                pe.wait_ge(s_a, 32)
                shift(0)
                pe.wait_ge(s_x, 16)
                for t in range(2):
                    turn_x(t)
                pe.wait_ge(arep_ready, 1)
                pe.wait_ge(xT_ready, 1)
                score_row(0, 0)
                pe.wait_ge(xT_ready, 2)
                score_row(0, 1)
                for t in range(2, NS):
                    turn_x(t)
                source_vectors()
                pe.wait_ge(xT_ready, NS)

            def wh_tiles(first, end):
                xcols = xT[:, :].rearrange("d (b c e) -> d b e c", b=NB, e=BYTES)
                for t in range(first, end):
                    b = t // WH_BANK
                    dst = acc[:, b - 1, :] if b else misc[:, :]
                    c = (t % WH_BANK) * E
                    last = nc.tensor.matmul(dst[:, c:c + E], xcols[:, t // BYTES, t % BYTES], wext1[:, :],
                                            start=True, stop=True)
                    if t % WH_BANK == WH_BANK - 1 or t == TILES - 1:
                        last.then_inc(tab_psum, 1)

            def tables1_early():
                pe.wait_ge(xT_ready, 2 * NS - 1)
                wh_tiles(0, WH_BANK)
                pe.wait_ge(acc_read, NS * RB + RB)
                wh_tiles(WH_BANK, TILES // 2)
                score_row(1, 0)

            def tables1():
                pe.wait_ge(xT_ready, 2 * NS)
                wh_tiles(TILES // 2, TILES)
                shift(1)
                score_row(1, 1)

            def granule(layer, s, g):
                k = (layer * NS + s) * NG + g
                pe.wait_ge(neg_ready, k + 1)
                pe.wait_ge(pos_ready, k + 1)
                pe.sem_inc(pe_turn, 1)
                pe.wait_ge(x_parts, layer * NG + g + 1)
                pe.wait_ge(y_parts, layer * NG + g + 1)
                masks = [m[:, g, :].bitcast(FP8).rearrange("p (b i e) -> p b e i", b=GB, e=BYTES) for m in (pos, neg)]
                for r in range(RB):
                    if g == 0:
                        pe.wait_ge(acc_read, (layer * NS + s) * RB + r + 1)
                    if g == 0:
                        pe.sem_inc(pe_turn, 1)
                    for t in range(GT):
                        for c in range(2):
                            last = nc.tensor.matmul(
                                acc[:, r, c * XW:(c + 1) * XW], masks[c][:, t // BYTES, t % BYTES, r * P:(r + 1) * P],
                                xy[layer][:, g * GT + t, c].rearrange("p k f -> p (k f)"),
                                start=(g == 0 and t == 0 and c == 0), stop=(g == NG - 1 and t == GT - 1),
                                skip_group_check=True)
                    last.then_inc(products, 1)

            def turn_x1(s):
                pe.wait_ge(x1_ready, s + 2)
                pe.wait_ge(xT_ready, NS + s)
                pe.sem_inc(pe_turn, 1)
                for b in range(RB):
                    last = nc.tensor.transpose(flip[0:D, b * P:(b + 1) * P], x1s[:, b, :], idf[:, :])
                last.then_inc(x1_turned, 1)

            def body(layer, s, last=False):
                granule(layer, s, NG - 1)
                if not last:
                    score_row(layer, s + 2)
                for g in range(NG - 1):
                    granule(layer, s + 1, g)
                if layer == 0:
                    turn_x1(s)

            for layer in range(2):
                [tables0, tables1][layer]()
                for g in range(NG - 1):
                    granule(layer, 0, g)
                    if g == 0:
                        mean(layer)
                with pe.Fori(0, NS - 2) as s:
                    body(layer, s)
                body(layer, NS - 2, last=True)
                granule(layer, NS - 1, NG - 1)
                if layer == 0:
                    tables1_early()
                    turn_x1(NS - 1)

        @block.scalar
        def _(act):
            act.sem_inc(x1_ready, 1)
            def tables0():
                act.wait_ge(s_h, 16 * NA + 16)
                nc.scalar.copy(wh[0][:, :, 0:D], h_raw.rearrange("p (t d) -> p t d", d=D)).then_inc(h_copied, 1)
                exps(0)
                for t in range(NS):
                    if t == 2:
                        signs(0, 0, 0)
                    act.wait_ge(xT_psum, t + 1)
                    nc.scalar.copy(xT_at(t), acc[0:D, t % RB, :].rearrange("d (r i) -> d r i", r=RB)).then_inc(xT_ready, 1)
                act.wait_ge(max_psum, 3)
                nc.scalar.copy(wT[:, :], misc[0:D, 0:D]).then_inc(w_ready, 1)

            def copy_wh(b):
                t0, t1 = b * WH_BANK, min((b + 1) * WH_BANK, TILES)
                src = (acc[:, b - 1, :] if b else misc[:, :])[:, 0:(t1 - t0) * E]
                act.wait_ge(tab_psum, b + 1)
                nc.scalar.copy(wh[1][:, t0:t1, :].rearrange("p t f -> p (t f)"), src).then_inc(tab_ready, 1)

            def tables1():
                for b in range(2, RB + 1):
                    copy_wh(b)
                signs(1, 0, 0, between=exps)

            def exps(layer):
                act.wait_ge(shift_ready, 2 * layer + 1)
                nc.scalar.activation(wts[:, layer, 0, :], dcol[:, layer, :], ACT.Exp, bias=mcol[:, 2:3]).then_inc(exp_ready, 1)
                nc.scalar.activation(wts[:, layer, 1, :], dcol[:, layer, :], ACT.Exp, bias=mcol[:, 3:4],
                                     scale=SLOPE).then_inc(exp_ready, 1)

            def row_factors(layer):
                act.wait_ge(shift_ready, 2 * layer + 2)
                nc.scalar.activation(ab[:, layer, :, :], ab[:, layer, :, :], ACT.Exp).then_inc(exp_ready, 1)

            def signs(layer, s, g, between=None):
                k = (layer * NS + s) * NG + g
                if g == 0:
                    if isinstance(s, int) and s == 0:
                        act.wait_ge(max_step, 2 * layer + 1)
                    act.wait_ge(srow_ready, layer * NS + s + 1)
                act.wait_ge(products, (k + 1) * RB)
                act.sem_inc(act_turn, 1)
                o = neg[:, g, :].bitcast(I8).rearrange("p (b i e) -> p b e i", b=GB, e=BYTES)
                for t in range(GT):
                    if between and t == GT // 2:
                        between(layer)
                    col = g * GT + t
                    last = nc.scalar.activation(o[:, t // BYTES, t % BYTES, :], srow[:, bass.ds((s % 2) * 512, 512)],
                                                ACT.Sign, bias=dcol[:, layer, col:col + 1])
                last.then_inc(signs_ready, 1)

            def normalize(layer, s):
                k = layer * NS + s
                act.wait_ge(std_ready, 2 * k + 2)
                if layer == 0:
                    act.wait_ge(x1_turned, s + 1)
                    act.wait_ge(x1_kept, s + 1)
                else:
                    act.wait_ge(stored, 16 * (s + 1))
                act.sem_inc(act_turn, 1)
                for r in range(RB):
                    last = nc.scalar.activation(x1s[:, r, :], y[:, r, :], ACT.Identity, bias=shift_n[:, r:r + 1],
                                                scale=rstd[:, r:r + 1])
                last.then_inc(x1_ready, 1)

            def copy_x1(s):
                act.wait_ge(x1_turned, s + 2)
                act.sem_inc(act_turn, 1)
                nc.scalar.copy(xT_at(s), flip[0:D, :].rearrange("d (r i) -> d r i", r=RB)).then_inc(xT_ready, 1)

            for layer in range(2):
                [tables0, tables1][layer]()
                for g in range(1, NG):
                    signs(layer, 0, g)
                row_factors(layer)
                signs(layer, 1, 0)
                with act.Fori(0, NS - 2) as s:
                    for g in range(1, NG):
                        signs(layer, s + 1, g)
                    normalize(layer, s)
                    signs(layer, s + 2, 0)
                    if layer == 0:
                        copy_x1(s)
                for g in range(1, NG):
                    signs(layer, NS - 1, g)
                normalize(layer, NS - 2)
                if layer == 0:
                    copy_x1(NS - 2)
                    copy_wh(0)
                    copy_wh(1)
                normalize(layer, NS - 1)
                if layer == 0:
                    copy_x1(NS - 1)

        @block.vector
        def _(dve):
            dve.sem_inc(acc_read, RB)
            pre = [0]

            def step(ins):
                pre[0] += 1
                ins.then_inc(dve_pre, 1)
                dve.wait_ge(dve_pre, pre[0])

            nc.vector.memset(onesN[:, :], 1.0 / N).then_inc(const_ready, 1)
            nc.vector.memset(one_row[:, :], 1.0).then_inc(const_ready, 1)
            nc.vector.memset(minus_half[:, :], -0.5).then_inc(const_ready, 1)
            dve.wait_ge(s_a, 32)
            nc.vector.tensor_copy(arep[:, 0, :], acol[:, 0:1].broadcast_to((D, P))).then_inc(arep_ready, 1)

            def source_vectors():
                dve.wait_ge(max_psum, 4)
                nc.vector.tensor_copy(arep[:, 1, :], misc[0:D, 64:65].broadcast_to((D, P))).then_inc(w_ready, 1)
                nc.vector.tensor_copy(wext1[:, D:E], misc[0:D, 65:66]).then_inc(w_ready, 1)
                dve.wait_ge(s_prod, 1)
                step(nc.vector.tensor_reduce(scol[:, 0, :], s_terms, AX, ALU.add))
                dve.wait_ge(max_psum, 5)
                nc.vector.tensor_copy(arow[:, 2 * D:3 * D], misc[:, 128:128 + D]).then_inc(w_ready, 1)

            def dots(col, table, k, temp):
                a = arow[:, k * D:(k + 1) * D].unsqueeze(1).broadcast_to((P, TILES, D))
                step(nc.vector.tensor_tensor(temp, table, a, ALU.mult))
                step(nc.vector.tensor_reduce(col, temp, AX, ALU.add))

            def tables(layer):
                w = wh[layer]
                if layer == 0:
                    dve.wait_ge(s_h, 16 * NA + 16)
                    dots(dcol[:, 0, :], h_raw.rearrange("p (t d) -> p t d", d=D), 1, prod[0][:, 1, :, 0:D])
                else:
                    dve.wait_ge(tab_ready, RB + 1)
                    step(nc.vector.tensor_copy(dcol[:, layer, :], w[:, :, D]))
                nc.vector.tensor_reduce(mcol[:, 0:1], dcol[:, layer, :], AX, ALU.max).then_inc(max_step, 1)
                step(nc.vector.memset(w[:, :, D:E], 1.0))
                dve.wait_ge(max_psum, 1 + 6 * layer)
                nc.vector.tensor_reduce(mcol[0:1, 1:2], flip[0:1, 128:256], AX, ALU.max).then_inc(max_step, 1)
                dve.wait_ge(max_psum, 2 + 6 * layer)
                step(nc.vector.tensor_scalar(mcol[:, 2:3], flip[:, 256:257], -1.0, None, ALU.mult))
                nc.vector.tensor_scalar(mcol[:, 3:4], mcol[:, 2:3], SLOPE, None, ALU.mult).then_inc(shift_ready, 1)
                dve.wait_ge(exp_ready, 3 * layer + 2)
                h = KEEP * GT
                nc.vector.tensor_scalar(wts[:, layer, :, h:TILES], wts[:, layer, :, h:TILES], RESCALE, None, ALU.mult)\
                  .then_inc(weights_ready, 1)
                dve.wait_ge(weights_ready, layer + 1)

            def column_sums():
                nc.vector.tensor_reduce(hsum[:, :], wh[1][:, :, 0:D].rearrange("p t f -> p f t"), AX, ALU.add)\
                  .then_inc(max_step, 1)

            def row_factors(layer):
                if layer == 0:
                    dve.wait_ge(max_psum, 6)
                else:
                    dve.wait_ge(x1_kept, NS + 1)
                    dve.wait_ge(x_parts, NG * 2)
                    dots(scol[:, layer, :], xn[:, :, :], 2, prod[layer][:, 0, :, 0:D])
                step(nc.vector.tensor_scalar(scol[:, layer, :], scol[:, layer, :], mcol[:, 2:3], None, ALU.subtract))
                nc.vector.tensor_scalar(ab[:, layer, 0, :], scol[:, layer, :], 1 - SLOPE, 0.0, ALU.mult, ALU.min)
                nc.vector.tensor_scalar(ab[:, layer, 1, :], scol[:, layer, :], SLOPE - 1, 0.0, ALU.mult, ALU.min)\
                  .then_inc(shift_ready, 1)
                if layer == 0:
                    step(nc.vector.tensor_reduce(meanv[:, 0, :], misc[:, :].rearrange("p (b d) -> p d b", d=D), AX, ALU.add))
                else:
                    dve.wait_ge(max_psum, 9)
                    step(nc.vector.tensor_copy(meanv[:, layer, :], misc[:, 448:448 + D]))

            def split_x(layer, g):
                t = slice(g * GT, (g + 1) * GT)
                r = prod[layer][:, 0, t, :]
                hi, mid, lo = (xy[layer][:, t, 0, part, :] for part in range(PARTS))
                step(nc.vector.tensor_tensor(r, wh[layer][:, t, :],
                                             wts[:, layer, 0, t].unsqueeze(2).broadcast_to((P, GT, E)), ALU.mult))
                step(nc.vector.tensor_copy(hi, r))
                step(nc.vector.tensor_tensor(r, r, hi, ALU.subtract))
                step(nc.vector.tensor_copy(mid, r))
                nc.vector.tensor_tensor(lo, r, mid, ALU.subtract).then_inc(x_parts, 1)

            def words(ap):
                return ap.bitcast(U32)

            def to_bytes(s, g):
                k = s * NG + g
                dve.wait_ge(loaded[g % SLOTS], 16 * NA * (s * (NG // SLOTS) + g // SLOTS + 1))
                if g != 0 or not isinstance(s, int):
                    dve.wait_ge(turned_ready, k)
                nc.vector.tensor_scalar(
                    narrow[:, :].rearrange("p (b g j) -> p g b j", b=GB, g=GR),
                    stage[:, g % SLOTS, :].rearrange("p (g b j) -> p g b j", g=GR, b=GB),
                    0.0, float(CODE[g // KEEP]), ALU.is_gt, ALU.mult).then_inc(narrowed, 1)

            def turn(s, g):
                k = s * NG + g
                dve.wait_ge(turned_kept, s * KEEP + g % KEEP + 1)
                if not isinstance(s, int) or s > 0:
                    dve.wait_ge(pos_ready, k - NG + 1)
                dve.wait_ge(narrowed, k + 1)
                nc.vector.transpose(words(turned[:, g, :]), words(narrow[:, :])).then_inc(turned_ready, 1)

            def mask(layer, s, g):
                k = (layer * NS + s) * NG + g
                c = words(neg[:, g, :])
                dve.wait_ge(signs_ready, k + 1)
                if layer == 0:
                    dve.wait_ge(turned_ready, s * NG + g + 1)
                    a = words(turned[:, g, :])
                    nc.vector.tensor_tensor(c, c, a, ALU.bitwise_and).then_inc(neg_ready, 1)
                else:
                    dve.wait_ge(turned_kept, NS * KEEP + KEEP)
                    a = words(kept_at(s, g))
                    nc.vector.scalar_tensor_tensor(c, a, BIT[g // KEEP], c, ALU.bitwise_and, ALU.bitwise_and)\
                      .then_inc(neg_ready, 1)
                    dve.wait_ge(neg_ready, k + 1)
                    nc.vector.scalar_tensor_tensor(words(pos[:, g, :]), a, BIT[g // KEEP], c, ALU.bitwise_and,
                                                   ALU.bitwise_xor).then_inc(pos_ready, 1)

            def read_acc(layer, s):
                for r in range(RB):
                    dve.wait_ge(products, FREE_AT_FIRST + ((layer * NS + s) * NG + NG - 1) * RB + r + 1)
                    nc.vector.tensor_reduce(
                        red[:, r, :, :].rearrange("p c f -> p (c f)").rearrange("p (c f) -> p c f", c=2),
                        acc[:, r, 0:2 * XW].rearrange("p (c k f) -> p c f k", c=2, k=PARTS), AX, ALU.add)\
                      .then_inc(acc_read, 1)

            def link(layer, s, n, ins):
                ins.then_inc(epi, 1)
                dve.wait_ge(epi, (layer * NS + s) * LINKS + n)

            V = nc.vector
            blocks = range(RB)

            def average(layer, s):
                row = [bass.ds(s * RB + r, 1) for r in blocks]
                dve.wait_ge(acc_read, (layer * NS + s) * RB + 2 * RB)
                dve.wait_ge(exp_ready, 3 * (layer + 1))
                link(layer, s, 1, [V.tensor_scalar(red[:, r, 1, :], red[:, r, 1, :], ab[:, layer, 1, row[r]], None,
                                                   ALU.mult) for r in blocks][-1])
                dve.wait_ge(x1_ready, layer * NS + s + 1)
                link(layer, s, 2, [V.scalar_tensor_tensor(num[:, r, :], red[:, r, 0, :], ab[:, layer, 0, row[r]],
                                                          red[:, r, 1, :], ALU.mult, ALU.add) for r in blocks][-1])
                link(layer, s, 3, V.tensor_scalar(empty, num[:, :, D], 0.0, None, ALU.is_equal))
                link(layer, s, 4, V.tensor_tensor(total, num[:, :, D], empty, ALU.add))
                V.reciprocal(rden, total).then_inc(epi, 1)

            def residual_sum(layer, s):
                dve.wait_ge(epi, (layer * NS + s) * LINKS + 5)
                dve.wait_ge(base_ready, layer * NS + s + 1)
                link(layer, s, 6, [V.scalar_tensor_tensor(y[:, r, :], y[:, r, :], rden[:, r:r + 1], base[:, r, :],
                                                          ALU.mult, ALU.add) for r in blocks][-1])
                link(layer, s, 7, [V.bn_stats(bn[:, r, :], y[:, r, :]) for r in blocks][-1])
                dve.sem_inc(dve_turn, 1)
                link(layer, s, 8, [V.bn_aggr(mv[:, r, :], bn[:, r, :]) for r in blocks][-1])
                V.tensor_scalar(minus_mean, mv[:, :, 0], -1.0, None, ALU.mult)
                V.tensor_scalar(var, mv[:, :, 1], EPS, None, ALU.add).then_inc(var_ready, 1)

            for layer in range(2):
                tables(layer)
                if layer == 0:
                    dve.wait_ge(h_copied, 1)
                split_x(layer, 0)
                if layer == 0:
                    split_x(0, 1)
                    to_bytes(0, 0)
                    turn(0, 0)
                for g in range(NG - 1):
                    mask(layer, 0, g)
                    if layer == 0:
                        if g == 0:
                            source_vectors()
                        to_bytes(0, g + 1)
                        turn(0, g + 1)
                    if layer == 1 and g == 0:
                        column_sums()
                    if g + 2 - layer < NG:
                        split_x(layer, g + 2 - layer)
                row_factors(layer)
                with dve.Fori(0, NS - 1) as s:
                    mask(layer, s, NG - 1)
                    for g in range(NG):
                        if layer == 0:
                            to_bytes(s + 1, g)
                        if g:
                            mask(layer, s + 1, g - 1)
                        if layer == 0:
                            turn(s + 1, g)
                        if g == 1:
                            read_acc(layer, s)
                        if g == 2:
                            average(layer, s)
                    residual_sum(layer, s)
                mask(layer, NS - 1, NG - 1)
                read_acc(layer, NS - 1)
                average(layer, NS - 1)
                residual_sum(layer, NS - 1)

        @block.gpsimd
        def _(pool):
            def inverse_std(layer, s):
                k = layer * NS + s
                pool.wait_ge(var_ready, k + 1)
                nc.gpsimd.tensor_tensor(rstd, var, minus_half[:, :], ALU.pow).then_inc(std_ready, 1)
                pool.wait_ge(std_ready, 2 * k + 1)
                pool.sem_inc(pool_turn, 1)
                nc.gpsimd.tensor_tensor(shift_n, minus_mean, rstd, ALU.mult).then_inc(std_ready, 1)

            def addends(layer, s):
                k = layer * NS + s
                pool.wait_ge(epi, k * LINKS + 3)
                pool.sem_inc(pool_turn, 1)
                nc.gpsimd.tensor_tensor(base, meanv[:, layer, :].unsqueeze(1).broadcast_to((P, RB, D)),
                                        empty.unsqueeze(2).broadcast_to((P, RB, D)), ALU.mult).then_inc(base_step, 1)
                n = 1
                if layer == 1:
                    pool.wait_ge(base_step, NS + 2 * s + n)
                    pool.sem_inc(pool_turn, 1)
                    nc.gpsimd.tensor_tensor(base, base, biasr[:, :].unsqueeze(1).broadcast_to((P, RB, D)), ALU.add)\
                      .then_inc(base_step, 1)
                    n = 2
                pool.wait_ge(base_step, layer * NS + (layer + 1) * s + n)
                pool.sem_inc(pool_turn, 1)
                nc.gpsimd.tensor_tensor(base, base, xn[:, bass.ds(s * RB, RB), :], ALU.add).then_inc(base_ready, 1)

            pre = [0]

            def step(ins):
                pre[0] += 1
                ins.then_inc(pool_pre, 1)
                pool.wait_ge(pool_pre, pre[0])

            def split_y(layer, g):
                t = slice(g * GT, (g + 1) * GT)
                r = prod[layer][:, 1, t, :]
                w = wts[:, layer, 1, t].unsqueeze(2).broadcast_to((P, GT, E))
                hi, mid, lo = (xy[layer][:, t, 1, part, :] for part in range(PARTS))
                nc.gpsimd.tensor_tensor(hi, wh[layer][:, t, :], w, ALU.mult)
                step(nc.gpsimd.tensor_tensor(r, wh[layer][:, t, :], w, ALU.mult))
                nc.gpsimd.tensor_tensor(mid, r, hi, ALU.subtract)
                step(nc.gpsimd.tensor_tensor(r, r, hi, ALU.subtract))
                nc.gpsimd.tensor_tensor(lo, r, mid, ALU.subtract).then_inc(y_parts, 1)

            def positive(s, g):
                pool.wait_ge(neg_ready, s * NG + g + 1)
                nc.gpsimd.tensor_tensor(pos[:, g, :].bitcast(U32), turned[:, g, :].bitcast(U32),
                                        neg[:, g, :].bitcast(U32), ALU.subtract).then_inc(pos_ready, 1)

            def keep(s, g):
                pool.wait_ge(turned_ready, s * NG + g + KEEP + 1)
                pool.sem_inc(pool_turn, 1)
                nc.gpsimd.tensor_tensor(kept_at(s, g).bitcast(U32), turned[:, g, :].bitcast(U32),
                                        turned[:, g + KEEP, :].bitcast(U32), ALU.add).then_inc(turned_kept, 1)

            pool.sem_inc(turned_kept, KEEP)
            pool.sem_inc(x1_kept, 1)

            def residual(s):
                pool.wait_ge(x1_ready, s + 2)
                pool.sem_inc(pool_turn, 1)
                nc.gpsimd.tensor_copy(xn[:, bass.ds(s * RB, RB), :], x1s[:, :, :]).then_inc(x1_kept, 1)

            pool.wait_ge(const_ready, 3)
            pool.wait_ge(s_h, 16 * NA + 16)
            pool.wait_ge(s_x, 16)
            nc.gpsimd.tensor_tensor(s_terms, xn[:, :, :], arow[:, 0:D].unsqueeze(1).broadcast_to((P, IB, D)),
                                    ALU.mult).then_inc(s_prod, 1)
            pool.wait_ge(h_copied, 1)
            pool.wait_ge(weights_ready, 1)
            split_y(0, 0)
            positive(0, 0)
            split_y(0, 1)
            positive(0, 1)
            split_y(0, 2)
            keep(0, 0)
            positive(0, 2)
            split_y(0, 3)
            with pool.Fori(0, NS - 1) as s:
                positive(s, 3)
                keep(s, 1)
                positive(s + 1, 0)
                positive(s + 1, 1)
                keep(s + 1, 0)
                addends(0, s)
                positive(s + 1, 2)
                inverse_std(0, s)
                residual(s)
            positive(NS - 1, 3)
            keep(NS - 1, 1)
            addends(0, NS - 1)
            inverse_std(0, NS - 1)
            residual(NS - 1)
            pool.wait_ge(weights_ready, 2)
            for g in range(NG):
                split_y(1, g)
            pool.wait_ge(s_bias, 16)
            with pool.Fori(0, NS) as s:
                addends(1, s)
                inverse_std(1, s)


_INS = ["x", "adj", "L0_gnn_a", "L1_gnn_weight_w", "L1_gnn_weight_a", "L1_gnn_bias"]


def kernel(**inputs):
    import concourse.bacc as bacc
    from concourse.bass_utils import run_bass_kernel_spmd as run

    nc = bacc.Bacc("TRN2", target_bir_lowering=False, num_devices=1)
    arrays, args = {}, []
    for name in _INS:
        a = np.ascontiguousarray(inputs[name])
        arrays[f"in_{name}"] = a
        args.append(nc.dram_tensor(f"in_{name}", a.shape, mybir.dt.from_np(a.dtype), kind="ExternalInput").ap())
    arrays["identity"] = np.eye(P, dtype=np.float32)
    args.append(nc.dram_tensor("identity", (P, P), F32, kind="ExternalInput").ap())
    out = nc.dram_tensor("out", arrays["in_x"].shape, F32, kind="ExternalOutput").ap()
    gat_kernel(nc, *args, out)
    r = run(nc, [arrays], core_ids=[0])
    return r.results[0]["out"]
```
